# Optimizing a Trainium2 kernel written in Bass

```python
import numpy as np
import jax
import jax.numpy as jnp

def _softmax(x, axis=-1):
    return jax.nn.softmax(x, axis=axis)

def _gelu(x):
    return jax.nn.gelu(x, approximate=True)

def _silu(x):
    return jax.nn.silu(x)

def _sigmoid(x):
    return jax.nn.sigmoid(x)

def _layernorm(x, axis=-1, eps=1e-05):
    m = jnp.mean(x, axis=axis, keepdims=True)
    v = jnp.var(x, axis=axis, keepdims=True)
    return (x - m) / jnp.sqrt(v + eps)

def _scatter_add(tgt, idx, src, axis=0):
    return tgt.at[idx].add(src)

def _segment_sum(src, seg, n):
    return jax.ops.segment_sum(src, seg, n)
kernel_name = 'mk_prb_d2_jaxref_r4_0341c4'

def setup_inputs(seed: int=0):
    np.random.seed(seed)
    _w = jnp.asarray

    def _L0_attn_setup():
        import jax, jax.numpy as jnp
        import numpy as np
        BLOCK = 128
        NUM_GLOBAL = 16
        GBL = BLOCK // NUM_GLOBAL
        NEG = -10000.0
        E = 256
        H = 16

        def _sparse_attn(q, k, v, M):
            B, Hn, S, d = q.shape
            nb = S // BLOCK
            rem = S % BLOCK
            Lg = S - S % GBL
            ns = Lg // GBL
            scale = 1.0 / jnp.sqrt(jnp.asarray(d, q.dtype))
            k_str = k[:, :, :Lg].reshape(B, Hn, ns, GBL, d)[:, :, :, -1, :]
            v_str = v[:, :, :Lg].reshape(B, Hn, ns, GBL, d)[:, :, :, -1, :]
            outs = []
            if nb > 0:
                L = nb * BLOCK
                fq = q[:, :, :L].reshape(B, Hn, nb, BLOCK, d)
                fk_loc = k[:, :, :L].reshape(B, Hn, nb, BLOCK, d)
                fv_loc = v[:, :, :L].reshape(B, Hn, nb, BLOCK, d)
                mloc = M[..., :L, :L].reshape(1, 1, nb, BLOCK, nb, BLOCK)
                mloc = jnp.moveaxis(jnp.diagonal(mloc, axis1=2, axis2=4), -1, 2)
                mstr = M[..., :L, :Lg].reshape(1, 1, nb, BLOCK, ns, GBL)[..., -1]
                fmask = jnp.concatenate([mstr, mloc], axis=-1)
                fk = jnp.concatenate([jnp.broadcast_to(k_str[:, :, None], (B, Hn, nb, ns, d)), fk_loc], axis=-2)
                fv = jnp.concatenate([jnp.broadcast_to(v_str[:, :, None], (B, Hn, nb, ns, d)), fv_loc], axis=-2)
                w = jnp.einsum('bhnqd,bhnkd->bhnqk', fq, fk) * scale + fmask
                w = jax.nn.softmax(w, axis=-1)
                o1 = jnp.einsum('bhnqk,bhnkd->bhnqd', w, fv).reshape(B, Hn, L, d)
                outs.append(o1)
            if rem > 0:
                sq = q[:, :, -rem:]
                sk = jnp.concatenate([k_str, k[:, :, -rem:]], axis=2)
                sv = jnp.concatenate([v_str, v[:, :, -rem:]], axis=2)
                mstr2 = M[..., -rem:, :Lg].reshape(1, 1, rem, ns, GBL)[..., -1]
                smask = jnp.concatenate([mstr2, M[..., -rem:, -rem:]], axis=-1)
                w2 = jnp.einsum('bhqd,bhkd->bhqk', sq, sk) * scale + smask
                w2 = jax.nn.softmax(w2, axis=-1)
                o2 = jnp.einsum('bhqk,bhkd->bhqd', w2, sv)
                outs.append(o2)
            return jnp.concatenate(outs, axis=-2) if len(outs) > 1 else outs[0]
        key = jax.random.key(seed)
        ks = jax.random.split(key, 4)
        B, S = (4, 576)
        return {'hidden_states': jax.random.normal(ks[0], (B, S, E), dtype=jnp.float32), 'c_attn_w': jax.random.normal(ks[1], (E, 3 * E), dtype=jnp.float32) * 0.02, 'c_attn_b': jnp.zeros((3 * E,), dtype=jnp.float32), 'c_proj_w': jax.random.normal(ks[2], (E, E), dtype=jnp.float32) * 0.02, 'c_proj_b': jnp.zeros((E,), dtype=jnp.float32)}
    _L0_attn_in = _L0_attn_setup()

    def _L0_ffn_setup():
        import jax, jax.numpy as jnp
        import numpy as np
        FEATURES = 256
        D_IN = 256

        def fp8_gemm_optimized(x, input_scale, kernel, kernel_scale):
            s_in = input_scale[0]
            s_k = kernel_scale[0]
            x_q = (x.astype(jnp.float32) / s_in).astype(jnp.float8_e4m3fn)
            k_q = (kernel.astype(jnp.float32) / s_k).astype(jnp.float8_e4m3fn)
            y = jnp.dot(x_q.astype(jnp.float32), k_q.astype(jnp.float32), preferred_element_type=jnp.float32)
            return y * (s_in * s_k)
        key = jax.random.key(seed)
        kx, kk, kb = jax.random.split(key, 3)
        x = jax.random.normal(kx, (4, 2048, D_IN), dtype=jnp.float32)
        limit = np.sqrt(6.0 / (D_IN + FEATURES)).astype(np.float32)
        kernel = jax.random.uniform(kk, (D_IN, FEATURES), dtype=jnp.float32, minval=-limit, maxval=limit).astype(jnp.bfloat16)
        input_scale = jnp.ones((1,), dtype=jnp.float32)
        kernel_scale = jnp.ones((1,), dtype=jnp.float32)
        bias = jnp.zeros((FEATURES,), dtype=jnp.bfloat16)
        return {'x': x, 'kernel': kernel, 'input_scale': input_scale, 'kernel_scale': kernel_scale, 'bias': bias}
    _L0_ffn_in = _L0_ffn_setup()

    def _L1_attn_setup():
        import jax, jax.numpy as jnp
        import numpy as np
        import math
        N_HEAD = 16
        N_EMBD = 256
        HEAD_DIM = N_EMBD // N_HEAD
        ROPE_BASE = 10000.0

        def _rope_cos_sin(T, dh, dtype):
            inv_freq = 1.0 / ROPE_BASE ** (jnp.arange(0, dh, 2, dtype=jnp.float32) / dh)
            freqs = jnp.arange(T, dtype=jnp.float32)[:, None] * inv_freq[None, :]
            cos = jnp.repeat(jnp.cos(freqs), 2, axis=-1).astype(dtype)
            sin = jnp.repeat(jnp.sin(freqs), 2, axis=-1).astype(dtype)
            return (cos, sin)

        def _apply_rope(x, cos, sin):
            x_even = x[..., ::2]
            x_odd = x[..., 1::2]
            x_rot = jnp.stack((-x_odd, x_even), axis=-1).reshape(x.shape)
            return x * cos + x_rot * sin
        key = jax.random.key(seed)
        k1, k2, k3 = jax.random.split(key, 3)
        B, T, C = (2, 512, N_EMBD)
        x = jax.random.normal(k1, (B, T, C), dtype=jnp.float32)
        Wqkv = jax.random.normal(k2, (C, 3 * C), dtype=jnp.float32) * (1.0 / math.sqrt(C))
        Wproj = jax.random.normal(k3, (C, C), dtype=jnp.float32) * (1.0 / math.sqrt(C))
        return {'x': x, 'Wqkv': Wqkv, 'Wproj': Wproj}
    _L1_attn_in = _L1_attn_setup()

    def _L1_ffn_setup():
        import jax, jax.numpy as jnp
        import numpy as np
        DIM = 256
        HEADS = 16
        HD = DIM // HEADS
        M = 64
        E = 4
        K = 2
        HID = 512
        MID = 512
        LB = 0.01
        EPS = 1.1920929e-07

        def _rms(x, w):
            return x * jax.lax.rsqrt(jnp.mean(x * x, axis=-1, keepdims=True) + EPS) * w

        def _gelu(x):
            return jax.nn.gelu(x, approximate=False)
        key = jax.random.key(seed)
        ks = jax.random.split(key, 20)
        d = DIM
        w = lambda k, s: jax.random.normal(k, s, jnp.float32) * 0.02
        return {'x': jax.random.normal(ks[0], (4, 256, d), jnp.float32), 'n1_w': jnp.ones((d,), jnp.float32), 'n2_w': jnp.ones((d,), jnp.float32), 'wq': w(ks[1], (d, d)), 'wk': w(ks[2], (d, d)), 'wv': w(ks[3], (d, d)), 'wo': w(ks[4], (d, d)), 'qn_w': jnp.ones((HD,), jnp.float32), 'kn_w': jnp.ones((HD,), jnp.float32), 'gate_w': w(ks[5], (E, d)), 'e0_up': w(ks[6], (HID, d)), 'e0_down': w(ks[7], (d, HID)), 'e1_w1': w(ks[8], (HID, d)), 'e1_w2': w(ks[9], (HID, d)), 'e1_down': w(ks[10], (d, HID)), 'e2_l1': w(ks[11], (MID, d)), 'e2_l2': w(ks[12], (HID, MID)), 'e2_l3': w(ks[13], (MID, HID)), 'e2_l4': w(ks[14], (d, MID)), 'e3_down': w(ks[15], (d, d)), 'e3_up': w(ks[16], (HID, d)), 'e3_out': w(ks[17], (d, HID))}
    _L1_ffn_in = _L1_ffn_setup()
    _d = {'L0_attn_hidden_states': _L0_attn_in['hidden_states'], 'L0_attn_c_attn_w': _L0_attn_in['c_attn_w'], 'L0_attn_c_attn_b': _L0_attn_in['c_attn_b'], 'L0_attn_c_proj_w': _L0_attn_in['c_proj_w'], 'L0_attn_c_proj_b': _L0_attn_in['c_proj_b'], 'L0_ffn_kernel': _L0_ffn_in['kernel'], 'L0_ffn_input_scale': _L0_ffn_in['input_scale'], 'L0_ffn_kernel_scale': _L0_ffn_in['kernel_scale'], 'L0_ffn_bias': _L0_ffn_in['bias'], 'L1_attn_Wqkv': _L1_attn_in['Wqkv'], 'L1_attn_Wproj': _L1_attn_in['Wproj'], 'L1_ffn_n1_w': _L1_ffn_in['n1_w'], 'L1_ffn_n2_w': _L1_ffn_in['n2_w'], 'L1_ffn_wq': _L1_ffn_in['wq'], 'L1_ffn_wk': _L1_ffn_in['wk'], 'L1_ffn_wv': _L1_ffn_in['wv'], 'L1_ffn_wo': _L1_ffn_in['wo'], 'L1_ffn_qn_w': _L1_ffn_in['qn_w'], 'L1_ffn_kn_w': _L1_ffn_in['kn_w'], 'L1_ffn_gate_w': _L1_ffn_in['gate_w'], 'L1_ffn_e0_up': _L1_ffn_in['e0_up'], 'L1_ffn_e0_down': _L1_ffn_in['e0_down'], 'L1_ffn_e1_w1': _L1_ffn_in['e1_w1'], 'L1_ffn_e1_w2': _L1_ffn_in['e1_w2'], 'L1_ffn_e1_down': _L1_ffn_in['e1_down'], 'L1_ffn_e2_l1': _L1_ffn_in['e2_l1'], 'L1_ffn_e2_l2': _L1_ffn_in['e2_l2'], 'L1_ffn_e2_l3': _L1_ffn_in['e2_l3'], 'L1_ffn_e2_l4': _L1_ffn_in['e2_l4'], 'L1_ffn_e3_down': _L1_ffn_in['e3_down'], 'L1_ffn_e3_up': _L1_ffn_in['e3_up'], 'L1_ffn_e3_out': _L1_ffn_in['e3_out']}
    _x0 = _d['L0_attn_hidden_states']
    _d['L0_attn_hidden_states'] = jax.random.normal(jax.random.fold_in(jax.random.key(seed), 1), (1, 4096, 256), dtype=_x0.dtype)
    del _x0
    return _d

def reference(L0_attn_hidden_states, L0_attn_c_attn_w, L0_attn_c_attn_b, L0_attn_c_proj_w, L0_attn_c_proj_b, L0_ffn_kernel, L0_ffn_input_scale, L0_ffn_kernel_scale, L0_ffn_bias, L1_attn_Wqkv, L1_attn_Wproj, L1_ffn_n1_w, L1_ffn_n2_w, L1_ffn_wq, L1_ffn_wk, L1_ffn_wv, L1_ffn_wo, L1_ffn_qn_w, L1_ffn_kn_w, L1_ffn_gate_w, L1_ffn_e0_up, L1_ffn_e0_down, L1_ffn_e1_w1, L1_ffn_e1_w2, L1_ffn_e1_down, L1_ffn_e2_l1, L1_ffn_e2_l2, L1_ffn_e2_l3, L1_ffn_e2_l4, L1_ffn_e3_down, L1_ffn_e3_up, L1_ffn_e3_out):

    def _L0_attn_ref(hidden_states, c_attn_w, c_attn_b, c_proj_w, c_proj_b):
        import jax, jax.numpy as jnp
        import numpy as np
        BLOCK = 128
        NUM_GLOBAL = 16
        GBL = BLOCK // NUM_GLOBAL
        NEG = -10000.0
        E = 256
        H = 16

        def _sparse_attn(q, k, v, M):
            B, Hn, S, d = q.shape
            nb = S // BLOCK
            rem = S % BLOCK
            Lg = S - S % GBL
            ns = Lg // GBL
            scale = 1.0 / jnp.sqrt(jnp.asarray(d, q.dtype))
            k_str = k[:, :, :Lg].reshape(B, Hn, ns, GBL, d)[:, :, :, -1, :]
            v_str = v[:, :, :Lg].reshape(B, Hn, ns, GBL, d)[:, :, :, -1, :]
            outs = []
            if nb > 0:
                L = nb * BLOCK
                fq = q[:, :, :L].reshape(B, Hn, nb, BLOCK, d)
                fk_loc = k[:, :, :L].reshape(B, Hn, nb, BLOCK, d)
                fv_loc = v[:, :, :L].reshape(B, Hn, nb, BLOCK, d)
                mloc = M[..., :L, :L].reshape(1, 1, nb, BLOCK, nb, BLOCK)
                mloc = jnp.moveaxis(jnp.diagonal(mloc, axis1=2, axis2=4), -1, 2)
                mstr = M[..., :L, :Lg].reshape(1, 1, nb, BLOCK, ns, GBL)[..., -1]
                fmask = jnp.concatenate([mstr, mloc], axis=-1)
                fk = jnp.concatenate([jnp.broadcast_to(k_str[:, :, None], (B, Hn, nb, ns, d)), fk_loc], axis=-2)
                fv = jnp.concatenate([jnp.broadcast_to(v_str[:, :, None], (B, Hn, nb, ns, d)), fv_loc], axis=-2)
                w = jnp.einsum('bhnqd,bhnkd->bhnqk', fq, fk) * scale + fmask
                w = jax.nn.softmax(w, axis=-1)
                o1 = jnp.einsum('bhnqk,bhnkd->bhnqd', w, fv).reshape(B, Hn, L, d)
                outs.append(o1)
            if rem > 0:
                sq = q[:, :, -rem:]
                sk = jnp.concatenate([k_str, k[:, :, -rem:]], axis=2)
                sv = jnp.concatenate([v_str, v[:, :, -rem:]], axis=2)
                mstr2 = M[..., -rem:, :Lg].reshape(1, 1, rem, ns, GBL)[..., -1]
                smask = jnp.concatenate([mstr2, M[..., -rem:, -rem:]], axis=-1)
                w2 = jnp.einsum('bhqd,bhkd->bhqk', sq, sk) * scale + smask
                w2 = jax.nn.softmax(w2, axis=-1)
                o2 = jnp.einsum('bhqk,bhkd->bhqd', w2, sv)
                outs.append(o2)
            return jnp.concatenate(outs, axis=-2) if len(outs) > 1 else outs[0]
        B, S, Em = hidden_states.shape
        d = Em // H
        qkv = hidden_states @ c_attn_w + c_attn_b
        q, k, v = jnp.split(qkv, 3, axis=-1)

        def split_heads(t):
            return t.reshape(B, S, H, d).transpose(0, 2, 1, 3)
        q, k, v = (split_heads(q), split_heads(k), split_heads(v))
        causal = jnp.tril(jnp.ones((S, S), dtype=bool))
        M = jnp.where(causal, 0.0, NEG).astype(hidden_states.dtype)[None, None]
        attn_out = _sparse_attn(q, k, v, M)
        attn_out = attn_out.transpose(0, 2, 1, 3).reshape(B, S, Em)
        return attn_out @ c_proj_w + c_proj_b

    def _L0_ffn_ref(x, kernel, input_scale, kernel_scale, bias):
        import jax, jax.numpy as jnp
        import numpy as np
        FEATURES = 256
        D_IN = 256

        def fp8_gemm_optimized(x, input_scale, kernel, kernel_scale):
            s_in = input_scale[0]
            s_k = kernel_scale[0]
            x_q = (x.astype(jnp.float32) / s_in).astype(jnp.float8_e4m3fn)
            k_q = (kernel.astype(jnp.float32) / s_k).astype(jnp.float8_e4m3fn)
            y = jnp.dot(x_q.astype(jnp.float32), k_q.astype(jnp.float32), preferred_element_type=jnp.float32)
            return y * (s_in * s_k)
        dtype = jnp.bfloat16
        x = x.astype(dtype)
        orig_shape = x.shape
        x2 = x.reshape(-1, x.shape[-1])
        y = fp8_gemm_optimized(x2, input_scale, kernel, kernel_scale)
        y = y.astype(dtype) + bias
        return y.reshape(orig_shape[:-1] + (FEATURES,))

    def _L1_attn_ref(x, Wqkv, Wproj):
        import jax, jax.numpy as jnp
        import numpy as np
        import math
        N_HEAD = 16
        N_EMBD = 256
        HEAD_DIM = N_EMBD // N_HEAD
        ROPE_BASE = 10000.0

        def _rope_cos_sin(T, dh, dtype):
            inv_freq = 1.0 / ROPE_BASE ** (jnp.arange(0, dh, 2, dtype=jnp.float32) / dh)
            freqs = jnp.arange(T, dtype=jnp.float32)[:, None] * inv_freq[None, :]
            cos = jnp.repeat(jnp.cos(freqs), 2, axis=-1).astype(dtype)
            sin = jnp.repeat(jnp.sin(freqs), 2, axis=-1).astype(dtype)
            return (cos, sin)

        def _apply_rope(x, cos, sin):
            x_even = x[..., ::2]
            x_odd = x[..., 1::2]
            x_rot = jnp.stack((-x_odd, x_even), axis=-1).reshape(x.shape)
            return x * cos + x_rot * sin
        B, T, C = x.shape
        H, Dh = (N_HEAD, HEAD_DIM)
        qkv = x @ Wqkv
        q, k, v = jnp.split(qkv, 3, axis=-1)
        Q = q.reshape(B, T, H, Dh).transpose(0, 2, 1, 3)
        K = k.reshape(B, T, H, Dh).transpose(0, 2, 1, 3)
        V = v.reshape(B, T, H, Dh).transpose(0, 2, 1, 3)
        cos, sin = _rope_cos_sin(T, Dh, x.dtype)
        Q = _apply_rope(Q, cos, sin)
        K = _apply_rope(K, cos, sin)
        scores = jnp.einsum('bhqd,bhkd->bhqk', Q, K) / math.sqrt(Dh)
        causal = jnp.tril(jnp.ones((T, T), dtype=bool))
        scores = jnp.where(causal, scores, jnp.finfo(scores.dtype).min)
        attn = jax.nn.softmax(scores, axis=-1)
        y = jnp.einsum('bhqk,bhkd->bhqd', attn, V)
        y = y.transpose(0, 2, 1, 3).reshape(B, T, C)
        return y @ Wproj

    def _L1_ffn_ref(x, n1_w, n2_w, wq, wk, wv, wo, qn_w, kn_w, gate_w, e0_up, e0_down, e1_w1, e1_w2, e1_down, e2_l1, e2_l2, e2_l3, e2_l4, e3_down, e3_up, e3_out):
        import jax, jax.numpy as jnp
        import numpy as np
        DIM = 256
        HEADS = 16
        HD = DIM // HEADS
        M = 64
        E = 4
        K = 2
        HID = 512
        MID = 512
        LB = 0.01
        EPS = 1.1920929e-07

        def _rms(x, w):
            return x * jax.lax.rsqrt(jnp.mean(x * x, axis=-1, keepdims=True) + EPS) * w

        def _gelu(x):
            return jax.nn.gelu(x, approximate=False)
        B, T, C = x.shape
        h = _rms(x, n1_w)
        heads = lambda w_: (h @ w_.T).reshape(B, T, HEADS, HD).transpose(0, 2, 1, 3)
        q = _rms(heads(wq), qn_w)
        k = _rms(heads(wk), kn_w)
        v = heads(wv)
        scores = jnp.einsum('bhqd,bhkd->bhqk', q, k) * HD ** (-0.5)
        causal = jnp.tril(jnp.ones((T, T), bool))
        scores = jnp.where(causal[None, None], scores, -jnp.inf)
        attn = jax.nn.softmax(scores, axis=-1)
        ao = jnp.einsum('bhqk,bhkd->bhqd', attn, v).transpose(0, 2, 1, 3).reshape(B, T, C) @ wo.T
        ao = ao.at[:, :, :M].set(0.0)
        x = x + ao
        xf = _rms(x, n2_w).reshape(-1, C)
        N = xf.shape[0]
        logits = jnp.nan_to_num(xf @ gate_w.T)
        probs = jax.nn.softmax(logits, axis=-1)
        topv, topi = jax.lax.top_k(probs, K)
        topv = topv / (topv.sum(-1, keepdims=True) + 1e-08)
        wts = jnp.zeros((N, E), x.dtype).at[jnp.arange(N)[:, None], topi].add(topv)
        o0 = _gelu(xf @ e0_up.T) @ e0_down.T
        o1 = jax.nn.silu(xf @ e1_w1.T) * (xf @ e1_w2.T) @ e1_down.T
        o2 = _gelu(_gelu(_gelu(xf @ e2_l1.T) @ e2_l2.T) @ e2_l3.T) @ e2_l4.T
        o3 = _gelu(_gelu(xf @ e3_down.T) @ e3_up.T) @ e3_out.T
        moe = wts[:, 0:1] * o0 + wts[:, 1:2] * o1 + wts[:, 2:3] * o2 + wts[:, 3:4] * o3
        moe = moe.reshape(B, T, C).at[:, :, :M].set(0.0)
        return x + moe
    x = L0_attn_hidden_states
    xn = _layernorm(x, axis=-1)
    x = x + _L0_attn_ref(xn, L0_attn_c_attn_w, L0_attn_c_attn_b, L0_attn_c_proj_w, L0_attn_c_proj_b) + _L0_ffn_ref(xn, L0_ffn_kernel, L0_ffn_input_scale, L0_ffn_kernel_scale, L0_ffn_bias)
    xn = _layernorm(x, axis=-1)
    x = x + _L1_attn_ref(xn, L1_attn_Wqkv, L1_attn_Wproj) + _L1_ffn_ref(xn, L1_ffn_n1_w, L1_ffn_n2_w, L1_ffn_wq, L1_ffn_wk, L1_ffn_wv, L1_ffn_wo, L1_ffn_qn_w, L1_ffn_kn_w, L1_ffn_gate_w, L1_ffn_e0_up, L1_ffn_e0_down, L1_ffn_e1_w1, L1_ffn_e1_w2, L1_ffn_e1_down, L1_ffn_e2_l1, L1_ffn_e2_l2, L1_ffn_e2_l3, L1_ffn_e2_l4, L1_ffn_e3_down, L1_ffn_e3_up, L1_ffn_e3_out)
    return x

_drawn_inputs = setup_inputs


def setup_inputs(seed=0):
    import zlib

    import numpy as np

    out = dict(_drawn_inputs(seed))
    spreads = {'L0_attn_c_attn_b': (0.0, 0.327),
     'L0_attn_c_proj_b': (0.0, 0.1),
     'L1_ffn_n1_w': (1.0, 0.6),
     'L1_ffn_n2_w': (1.0, 0.6),
     'L1_ffn_qn_w': (1.0, 0.6),
     'L1_ffn_kn_w': (1.0, 0.6)}
    factors = {'L0_attn_c_attn_w': 8.0,
     'L1_ffn_wq': 8.0,
     'L1_ffn_wk': 8.0,
     'L1_ffn_wv': 8.0,
     'L1_ffn_wo': 8.0,
     'L1_ffn_gate_w': 7.227,
     'L1_ffn_e0_up': 5.491,
     'L1_ffn_e0_down': 5.388,
     'L1_ffn_e1_w1': 8.0,
     'L1_ffn_e1_w2': 8.0,
     'L1_ffn_e1_down': 8.0,
     'L1_ffn_e2_l1': 8.0,
     'L1_ffn_e2_l2': 8.0,
     'L1_ffn_e2_l3': 8.0,
     'L1_ffn_e2_l4': 8.0,
     'L1_ffn_e3_down': 8.0,
     'L1_ffn_e3_up': 8.0,
     'L1_ffn_e3_out': 8.0,
     'L1_attn_Wqkv': 8.0,
     'L1_attn_Wproj': 8.0}
    for name, (base, spread) in spreads.items():
        noise = np.random.default_rng([zlib.crc32(name.encode()), seed]).standard_normal(out[name].shape)
        drawn = base * np.exp(spread * noise) if base else spread * noise
        out[name] = jnp.asarray(drawn.astype(out[name].dtype))
    for name, factor in factors.items():
        out[name] = (out[name] * factor).astype(out[name].dtype)
    return out
```

```python
from contextlib import ExitStack

import numpy as np

import concourse.bass as bass
from concourse import mybir

F32 = mybir.dt.float32
BF16 = mybir.dt.bfloat16
F16 = mybir.dt.float16
U32 = mybir.dt.uint32
ALU = mybir.AluOpType
ACT = mybir.ActivationFunctionType
AX = mybir.AxisListType

P = 128
TOKENS, DIM = 4096, 256
HEADS, HEAD_DIM = 16, 16
STRIP = 512
STRIPS = TOKENS // STRIP
BLOCKS = STRIP // P
DC = DIM // P
GROUP = 4
GROUPS = HEADS // GROUP
GCOL = 32
TERMS = ((0, 0), (0, 1), (1, 0), (1, 1), (0, 2), (2, 0))
TROWS = len(TERMS) * HEAD_DIM
MROWS = 3
SCALE = HEAD_DIM ** -0.5
STRIDE = 8
NSTR = TOKENS // STRIDE
NEG0 = -10000.0 / SCALE
NEG1 = -1e30
LN_EPS = 1e-5
RMS_EPS = 1.1920929e-07
MASKED = 64
KEPT = DIM - MASKED
QK = 2 * DIM
FP8_FIRST_NAN = 480.0
EXPERTS = 4


class Signal:

    def __init__(self, nc, ctx, name):
        self.sem, self.count = ctx.enter_context(nc.semaphore(name)), 0

    def mark(self, instruction, by=1):
        instruction.then_inc(self.sem, by)
        self.count += by
        return (self, self.count)


class Waiter:

    def __init__(self, engine):
        self.engine, self.seen = engine, {}

    def __call__(self, *marks):
        for mark in marks:
            if mark is None:
                continue
            signal, value = mark
            if self.seen.get(signal, 0) < value:
                self.engine.wait_ge(signal.sem, value)
                self.seen[signal] = value


class Slot:

    def __init__(self, tile, load_signal=None, store_signal=None):
        self.tile, self.load_signal, self.store_signal = tile, load_signal, store_signal
        self.readers, self.ready = [], None


class Ring:

    def __init__(self, slots):
        self.slots, self.at = slots, 0

    def take(self):
        slot = self.slots[self.at % len(self.slots)]
        self.at += 1
        old, slot.readers = slot.readers, []
        return slot, old


def spread(main, side, until=1.0):
    n = 0
    for i, step in enumerate(main):
        step()
        goal = min(len(side), int(len(side) * (i + 1) / max(1, until * len(main)) + 1e-9))
        while n < goal:
            side[n]()
            n += 1
    while n < len(side):
        side[n]()
        n += 1


def build(nc, d, out):
    ctx = ExitStack()
    with ctx:
        _build(nc, ctx, d, out)


def _build(nc, ctx, d, out):
    pe, dve, act, pool, sp = nc.tensor, nc.vector, nc.scalar, nc.gpsimd, nc.sync
    w_pe, w_dve, w_act, w_pool, w_sp = (Waiter(e) for e in (pe, dve, act, pool, sp))

    def signal(name):
        return Signal(nc, ctx, name)

    def sbuf(stack, name, shape, dt=F32):
        return stack.enter_context(nc.sbuf_tensor(name, shape, dt))

    def ring(stack, name, n, shape, dt=F32, loads=False, stores=False):
        slots = [Slot(sbuf(stack, f"{name}{i}", shape, dt), signal(f"{name}{i}_loaded") if loads else None,
                      signal(f"{name}{i}_stored") if stores else None) for i in range(n)]
        store_signals.extend(slot.store_signal for slot in slots if stores)
        return Ring(slots)

    def scratch(name, shape, dt=F32):
        return nc.dram_tensor(name, shape, dt).ap()

    pe_done = signal("pe_done")
    dve_done = signal("dve_done")
    act_done = signal("act_done")
    pool_done = signal("pool_done")
    store_signals = []

    def V(instruction):
        return dve_done.mark(instruction)

    def A(instruction):
        return act_done.mark(instruction)

    def G(instruction):
        return pool_done.mark(instruction)

    def T(instruction):
        return pe_done.mark(instruction)

    base_d = scratch("base_scratch", (TOKENS, DIM))
    x1_d = scratch("x1_scratch", (TOKENS, DIM))
    xn_d = scratch("xn_scratch", (TOKENS, DIM))
    parts_d = [[scratch(f"parts_scratch{a}_{s}", (QK, TOKENS), BF16) for s in range(3)] for a in range(3)]
    v_d = [scratch(f"v_scratch{a}", (GROUPS, TOKENS, GROUP * GCOL)) for a in range(3)]
    ao_d = [scratch(f"ao_scratch{a}", (TOKENS, DIM)) for a in range(3)]

    psum = ctx.enter_context(nc.psum_tensor("psum", [P, 8, 512], F32))

    const_in = signal("const_in")
    ident = sbuf(ctx, "ident", [P, P])
    ident_bf = sbuf(ctx, "ident_bf", [P, P], BF16)
    ident_h = sbuf(ctx, "ident_h", [P, P], F16)
    tri_key = sbuf(ctx, "tri_key", [P, P], BF16)
    tri_query = sbuf(ctx, "tri_query", [P, P], BF16)
    for tile, name in ((ident, "c_ident"), (ident_bf, "c_ident_bf"), (ident_h, "c_ident_h"),
                       (tri_key, "c_tri_key"), (tri_query, "c_tri_query")):
        consts = const_in.mark(sp.dma_start(tile[:], d[name]), 16)

    def rows_of(dram, strip):
        return dram[strip * STRIP:(strip + 1) * STRIP, :].rearrange("(b p) n -> p b n", p=P)

    stored = {}


    def norm_scale(small, var, eps):
        ve, sd, rs, t = (small[:, i, :] for i in range(4))
        m = V(dve.tensor_scalar(ve, var, eps, None, ALU.add))
        w_act(m)
        m = A(act.activation(sd, ve, ACT.Sqrt))
        w_dve(m)
        w_dve(V(dve.reciprocal(rs, sd)))
        w_dve(V(dve.tensor_tensor(t, rs, rs, ALU.mult)))
        w_dve(V(dve.tensor_tensor(t, t, ve, ALU.mult)))
        w_dve(V(dve.tensor_scalar(t, t, -0.5, 1.5, ALU.mult, ALU.add)))
        m = V(dve.tensor_tensor(rs, rs, t, ALU.mult))
        w_dve(m)
        return rs, m

    def layer_norm(x, xn, stats, small):
        st, mv = stats
        for b in range(BLOCKS):
            m = V(dve.bn_stats(st[:, b, :], x[:, b, :]))
        w_dve(m)
        for b in range(BLOCKS):
            m = V(dve.bn_aggr(mv[:, b, :], st[:, b, :]))
        w_dve(m)
        rs, _ = norm_scale(small, mv[:, :, 1], LN_EPS)
        for b in range(BLOCKS):
            m = V(dve.tensor_scalar(xn[:, b, :], x[:, b, :], mv[:, b, 0:1], rs[:, b:b + 1],
                                    ALU.subtract, ALU.mult))
        return m

    def mean_square(x, junk, ms):
        for b in range(BLOCKS):
            m = V(dve.tensor_tensor_reduce(out=junk[:], in0=x[:, b, :], in1=x[:, b, :], scale=1.0 / DIM,
                                           scalar=0.0, op0=ALU.mult, op1=ALU.add, accum_out=ms[:, b:b + 1]))
            w_dve(m)
        return m

    def to_features(x, ready, bank_ring, xt, xt_free):
        marks = []
        for c in range(DC):
            bank, readers = bank_ring.take()
            w_pe(ready, *readers)
            for b in range(BLOCKS):
                m = pe.transpose(bank.tile[:, b * P:(b + 1) * P], x[:, b, c * P:(c + 1) * P], ident[:])
            m = T(m)
            w_act(m, *xt_free)
            m = A(act.activation(xt[:, c, :], bank.tile, ACT.Copy))
            bank.readers.append(m)
            marks.append(m)
        return marks[-1]

    def bank_ring(ids):
        return Ring([Slot(psum[:, i, :], None) for i in ids])

    def make_parts(a, strip, qkn, ready, quad, quad_readers, parts_slot, parts_free):
        w_pe(ready, *quad_readers)
        for f in range(QK // P):
            for b in range(BLOCKS):
                m = pe.transpose(quad[:, f, b * P:(b + 1) * P], qkn[:, b, f * P:(f + 1) * P], ident[:])
        turned = T(m)
        p1, p2, p3, rest = parts_slot.tile
        w_act(turned, *parts_free)
        first = A(act.activation(p1[:], quad, ACT.Copy))
        w_dve(first)
        rested = V(dve.tensor_tensor(rest[:], quad, p1[:], ALU.subtract))
        w_pool(rested, *parts_free)
        second = G(pool.tensor_copy(p2[:], rest[:]))
        w_pool(second)
        third = G(pool.tensor_tensor(p3[:], rest[:], p2[:], ALU.subtract))
        w_sp(first, third)
        for s, part in enumerate((p1, p2, p3)):
            dst = parts_d[a][s][:, strip * STRIP:(strip + 1) * STRIP].rearrange("(m p) t -> p m t", p=P)
            kept = parts_slot.store_signal.mark(sp.dma_start(dst, part[:]), 16)
        return rested, kept, turned

    def store_v(a, strip, ve_slot, ready):
        w_sp(ready)
        for g in range(GROUPS):
            dst = v_d[a][g, strip * STRIP:(strip + 1) * STRIP, :].rearrange("(b p) n -> p b n", p=P)
            kept = ve_slot.store_signal.mark(sp.dma_start(dst, ve_slot.tile[:, :, g * GROUP * GCOL:(g + 1) * GROUP * GCOL]), 16)
        return kept

    def everyone_waits():
        last = [(s, s.count) for s in [pe_done, dve_done, act_done, pool_done] + store_signals if s.count]
        for w in (w_pe, w_dve, w_act, w_pool, w_sp):
            w(*last)


    with ExitStack() as st1:
        weights = signal("embed_weights")
        wqkv = sbuf(st1, "wqkv0", [P, DC, 3 * DIM])
        bqkv = sbuf(st1, "bqkv0", [P, 3 * DIM])
        bproj = sbuf(st1, "bproj0", [P, DIM])
        kraw = sbuf(st1, "fp8_w_raw", [P, DC, DIM], BF16)
        bias8 = sbuf(st1, "fp8_bias", [P, DIM], BF16)
        scales = sbuf(st1, "fp8_scales", [P, 2])
        weights.mark(sp.dma_start(wqkv[:], d["L0_attn_c_attn_w"].rearrange("(c p) n -> p c n", p=P)), 16)
        weights.mark(sp.dma_start(bqkv[:], d["L0_attn_c_attn_b"].partition_broadcast(P)), 16)
        weights.mark(sp.dma_start(bproj[:], d["L0_attn_c_proj_b"].partition_broadcast(P)), 16)
        weights.mark(sp.dma_start(kraw[:], d["L0_ffn_kernel"].rearrange("(c p) n -> p c n", p=P)), 16)
        weights.mark(sp.dma_start(bias8[:], d["L0_ffn_bias"].partition_broadcast(P)), 16)
        weights.mark(sp.dma_start(scales[:, 0:1], d["L0_ffn_input_scale"].partition_broadcast(P)), 16)
        w_in = weights.mark(sp.dma_start(scales[:, 1:2], d["L0_ffn_kernel_scale"].partition_broadcast(P)), 16)

        recip = sbuf(st1, "fp8_recip", [P, 2])
        product = sbuf(st1, "fp8_product", [P, 1])
        w_dve(w_in, consts)
        w_pool(w_in)
        V(dve.reciprocal(recip[:], scales[:]))
        m_scales = V(dve.tensor_tensor(product[:], scales[:, 0:1], scales[:, 1:2], ALU.mult))
        w_dve(m_scales)

        q8_a = sbuf(st1, "q8_a", [P, DC, STRIP])
        q8_b = sbuf(st1, "q8_b", [P, DC, STRIP])
        q8_c = sbuf(st1, "q8_c", [P, DC, STRIP])
        q8_x = sbuf(st1, "q8_x", [P, DC, STRIP], BF16)

        def round_fp8(src, scale_column, width, out_tile, free):
            a, b, c = (t[:, :, 0:width] for t in (q8_a, q8_b, q8_c))
            w_dve(*free, V(dve.tensor_scalar(a, src, recip[:, scale_column:scale_column + 1], None, ALU.mult)))
            w_dve(V(dve.tensor_scalar(b.bitcast(U32), a.bitcast(U32), 0x7F800000, None, ALU.bitwise_and)))
            w_dve(V(dve.tensor_scalar(b, b, 2.0 ** -6, 1.5 * 2.0 ** 20, ALU.max, ALU.mult)))
            w_dve(V(dve.tensor_tensor(a, a, b, ALU.add)))
            m = V(dve.tensor_tensor(a, a, b, ALU.subtract))
            w_dve(m)
            w_pool(m)
            w_pool(G(pool.tensor_tensor(c, a, a, ALU.mult)))
            w_pool(G(pool.tensor_scalar(c, c, FP8_FIRST_NAN ** 2, 3e38, ALU.is_ge, ALU.mult)))
            w_pool(G(pool.tensor_tensor(c, c, c, ALU.mult)))
            w_pool(G(pool.tensor_tensor(c, c, c, ALU.subtract)))
            w_pool(*free)
            m = G(pool.tensor_tensor(out_tile, a, c, ALU.add))
            return m

        kq = sbuf(st1, "fp8_w", [P, DC, DIM], BF16)
        m_kq = round_fp8(kraw[:], 1, DIM, kq[:], [])
        q8_free = [m_kq]

        xs = ring(st1, "x_in", 2, [P, BLOCKS, DIM], loads=True, stores=True)
        xns = ring(st1, "xn_s", 2, [P, BLOCKS, DIM])
        xts = ring(st1, "xt_s", 2, [P, DC, STRIP])
        xqs = ring(st1, "xq_s", 2, [P, DC, STRIP], BF16)
        qkns = ring(st1, "qkn_s", 2, [P, BLOCKS, QK])
        ves = ring(st1, "ve_s", 2, [P, BLOCKS, HEADS * GCOL], stores=True)
        yts = ring(st1, "y_s", 2, [P, DIM], BF16)
        stats = (sbuf(st1, "ln_stats", [P, BLOCKS, 6]), sbuf(st1, "ln_mv", [P, BLOCKS, 2]))
        small = sbuf(st1, "ln_small", [P, 4, BLOCKS])
        parts_ring = Ring([Slot(tuple(sbuf(st1, f"part{i}_{s}", [P, 4, STRIP], BF16) for s in range(3))
                                + (sbuf(st1, f"part{i}_r", [P, 4, STRIP]),), None, signal(f"parts_stored{i}")) for i in range(1)])
        store_signals.extend(slot.store_signal for slot in parts_ring.slots)
        for slot in ves.slots:
            slot.ready = V(dve.memset(slot.tile[:], 1.0))
        quads = Ring([Slot(psum[:, 0:4, :], None)])
        qk_banks, v_banks, t_banks = bank_ring((4, 5)), bank_ring((6,)), bank_ring((7,))

        def load_x(strip):
            slot, readers = xs.take()
            w_sp(*readers)
            slot.ready = slot.load_signal.mark(sp.dma_start(slot.tile[:], rows_of(d["L0_attn_hidden_states"], strip)), 16)
            return slot

        x_slot = load_x(0)
        for strip in range(STRIPS):
            x = x_slot
            if strip + 1 < STRIPS:
                x_slot = load_x(strip + 1)
            xn, xn_free = xns.take()
            w_dve(x.ready, *xn_free)
            normed = layer_norm(x.tile, xn.tile, stats, small)
            xt, xt_free = xts.take()
            turned = to_features(xn.tile, normed, t_banks, xt.tile, xt_free)
            xn.readers += [turned]
            w_dve(turned, *q8_free)
            xq, xq_free = xqs.take()
            w_dve(V(dve.tensor_copy(q8_x[:], xt.tile[:])))
            m_xq = round_fp8(q8_x[:], 0, STRIP, xq.tile[:], xq_free)
            q8_free = [m_xq]
            qkn, qkn_free = qkns.take()
            ve, ve_free = ves.take()
            w_pe(turned, w_in, consts)
            w_dve(*qkn_free, *ve_free)
            for b in range(BLOCKS):
                tok = slice(b * P, (b + 1) * P)
                bank, readers = qk_banks.take()
                w_pe(*readers)
                for c in range(DC):
                    m = pe.matmul(bank.tile, xt.tile[:, c, tok], wqkv[:, c, 0:QK], start=(c == 0), stop=(c == DC - 1))
                w_dve(T(m))
                m_qk = V(dve.tensor_tensor(qkn.tile[:, b, :], bank.tile, bqkv[:, 0:QK], ALU.add))
                bank.readers.append(m_qk)
                bank, readers = v_banks.take()
                w_pe(*readers)
                for c in range(DC):
                    m = pe.matmul(bank.tile[:, 0:DIM], xt.tile[:, c, tok], wqkv[:, c, QK:QK + DIM],
                                  start=(c == 0), stop=(c == DC - 1))
                m_mm = T(m)
                w_dve(m_mm)
                m_v = V(dve.tensor_tensor(
                    ve.tile[:, b, :].rearrange("p (h n) -> p h n", n=GCOL)[:, :, 0:HEAD_DIM],
                    bank.tile[:, 0:DIM].rearrange("p (h n) -> p h n", n=HEAD_DIM),
                    bqkv[:, QK:QK + DIM].rearrange("p (h n) -> p h n", n=HEAD_DIM), ALU.add))
                bank.readers.append(m_v)
            xt.readers += [m_mm]
            ve.readers.append(store_v(0, strip, ve, m_v))
            quad, quad_readers = quads.take()
            parts, parts_free = parts_ring.take()
            rested, kept, m_t = make_parts(0, strip, qkn.tile, m_qk, quad.tile, quad_readers, parts, parts_free)
            quad.readers.append(rested)
            parts.readers.append(kept)
            qkn.readers.append(m_t)
            for b in range(BLOCKS):
                bank, readers = v_banks.take()
                w_pe(m_xq, m_kq, *readers)
                for c in range(DC):
                    m = pe.matmul(bank.tile[:, 0:DIM], xq.tile[:, c, b * P:(b + 1) * P], kq[:, c, :],
                                  start=(c == 0), stop=(c == DC - 1))
                m = T(m)
                y, y_free = yts.take()
                w_dve(m, *y_free)
                m = V(dve.tensor_scalar(y.tile[:], bank.tile[:, 0:DIM], product[:, 0:1], None, ALU.mult))
                bank.readers.append(m)
                w_dve(m)
                w_dve(V(dve.tensor_tensor(y.tile[:], y.tile[:], bias8[:], ALU.add)))
                w_dve(V(dve.tensor_tensor(x.tile[:, b, :], x.tile[:, b, :], y.tile[:], ALU.add)))
                m = V(dve.tensor_tensor(x.tile[:, b, :], x.tile[:, b, :], bproj[:], ALU.add))
                y.readers.append(m)
            xq.readers.append((pe_done, pe_done.count))
            w_sp(m)
            x.readers.append(x.store_signal.mark(sp.dma_start(rows_of(base_d, strip), x.tile[:]), 16))
    everyone_waits()


    def attend(jobs, stage):
        units = [(a, g, j) for a in jobs for g in range(GROUPS) for j in range(STRIPS)]
        sparse = jobs == (0,)
        with ExitStack() as st:
            keys = ring(st, f"keys_{stage}_", 2, [TROWS + MROWS, GROUP, TOKENS], BF16, loads=True)
            values = ring(st, f"values_{stage}_", 2, [P, TOKENS // P, GROUP * GCOL], loads=True)
            queries = ring(st, f"queries_{stage}_", 3, [TROWS + MROWS, GROUP, STRIP], BF16, loads=True)
            probs = ring(st, f"probs_{stage}_", 6, [P, 2, STRIP])
            maxes = ring(st, f"maxes_{stage}_", 2, [P, GROUP * BLOCKS, STRIPS])
            neg = sbuf(st, f"neg_{stage}", [P, GROUP * BLOCKS])
            neg_rest = sbuf(st, f"neg_rest_{stage}", [P, GROUP * BLOCKS])
            neg_parts = ring(st, f"neg_parts_{stage}_", 2, [P, 3, GROUP * BLOCKS], BF16)
            neg_rows = ring(st, f"neg_rows_{stage}_", 2, [3 * GROUP * BLOCKS, P], BF16)
            outs = ring(st, f"outs_{stage}_", 2, [P, STRIP])
            recips = ring(st, f"recips_{stage}_", 2, [P, BLOCKS, GROUP])
            aos = ring(st, f"aos_{stage}_", 2, [P, BLOCKS, GROUP * HEAD_DIM], stores=True)
            mask_signal = signal(f"masks_{stage}")
            if sparse:
                str_values = ring(st, "str_values_", 2, [P, NSTR // P, GROUP * GCOL], loads=True)
                mask_q = sbuf(st, "mask_q", [P, (TOKENS - P) // STRIDE + NSTR], F16)
                mask_k = sbuf(st, "mask_k", [P, 3 * STRIP], F16)
                tri0_q = sbuf(st, "tri0_q", [P, STRIP], F16)
                tri0_k = sbuf(st, "tri0_k", [P, STRIP], F16)
                for tile, name in ((mask_q, "c_mask_q"), (mask_k, "c_mask_k"), (tri0_q, "c_tri0_q"), (tri0_k, "c_tri0_k")):
                    masks = mask_signal.mark(sp.dma_start(tile[:], d[name]), 16)
                w_pe(masks)
            ones = None
            for slot in keys.slots:
                ones = V(dve.memset(slot.tile[TROWS:TROWS + MROWS, :, :], 1.0))
            w_pe(ones)
            score_pairs = Ring([Slot(psum[:, 0:2, :], None), Slot(psum[:, 2:4, :], None)])
            pv_banks, side_banks = bank_ring((4, 5)), bank_ring((6, 7))
            group_buffers, unit_state = {}, {}

            def load(u):
                a, g, j = u
                if (a, g) not in group_buffers:
                    k, k_readers = keys.take()
                    v, v_readers = values.take()
                    w_sp(*k_readers, *v_readers)
                    for n, (_, part) in enumerate(TERMS):
                        src = parts_d[a][part][DIM + g * GROUP * HEAD_DIM:DIM + (g + 1) * GROUP * HEAD_DIM, :]
                        k.ready = k.load_signal.mark(sp.dma_start(
                            k.tile[n * HEAD_DIM:(n + 1) * HEAD_DIM, :, :],
                            src.rearrange("(h e) t -> e h t", e=HEAD_DIM)), 16)
                    v.ready = v.load_signal.mark(sp.dma_start(
                        v.tile[:], v_d[a][g].rearrange("(b p) n -> p b n", p=P)), 16)
                    sv = None
                    if sparse:
                        sv, sv_readers = str_values.take()
                        w_sp(*sv_readers)
                        sv.ready = sv.load_signal.mark(sp.dma_start(
                            sv.tile[:], v_d[a][g].rearrange("(c p e) n -> p c e n", p=P, e=STRIDE)[:, :, STRIDE - 1, :]), 16)
                    group_buffers[(a, g)] = (k, v, sv)
                q, q_readers = queries.take()
                w_sp(*q_readers)
                for n, (part, _) in enumerate(TERMS):
                    src = parts_d[a][part][g * GROUP * HEAD_DIM:(g + 1) * GROUP * HEAD_DIM, j * STRIP:(j + 1) * STRIP]
                    q.ready = q.load_signal.mark(sp.dma_start(
                        q.tile[n * HEAD_DIM:(n + 1) * HEAD_DIM, :, :],
                        src.rearrange("(h e) t -> e h t", e=HEAD_DIM)), 16)
                unit_state[u] = q

            def max_steps(u):
                a, g, j = u
                k, v, sv = group_buffers[(a, g)]
                q = unit_state[u]
                mx, mx_free = maxes.take()
                steps = []

                def tile_dense(h, b, kc):
                    def run():
                        bank, readers = side_banks.take()
                        w_pe(k.ready, q.ready, *readers)
                        diagonal = kc == j
                        width = (b + 1) * P if diagonal else STRIP
                        m = pe.matmul(bank.tile[:, 0:width], q.tile[0:TROWS, h, b * P:(b + 1) * P],
                                      k.tile[0:TROWS, h, kc * STRIP:kc * STRIP + width], start=True, stop=not diagonal)
                        if diagonal:
                            m = pe.matmul(bank.tile[:, b * P:(b + 1) * P], ident_bf[:], tri_query[:], start=False, stop=True)
                        w_dve(T(m), *mx_free)
                        m = V(dve.tensor_reduce(mx.tile[:, h * BLOCKS + b, kc:kc + 1], bank.tile[:, 0:width], AX.X, ALU.max))
                        bank.readers.append(m)
                    return run

                def tile_strided(h, b):
                    def run():
                        bank, readers = side_banks.take()
                        w_pe(k.ready, q.ready, *readers)
                        pe.matmul(bank.tile, q.tile[0:TROWS, h, b * P:(b + 1) * P],
                                  k.tile[0:TROWS, h, STRIDE - 1::STRIDE], start=True, stop=False)
                        first = (TOKENS - P) // STRIDE - (BLOCKS * j + b) * P // STRIDE
                        m = pe.matmul(bank.tile, ident_h[:], mask_q[:, first:first + NSTR], start=False, stop=True)
                        w_dve(T(m), *mx_free)
                        m = V(dve.tensor_reduce(mx.tile[:, h * BLOCKS + b, 0:1], bank.tile, AX.X, ALU.max))
                        bank.readers.append(m)
                    return run

                def tile_local(b):
                    def run():
                        bank, readers = side_banks.take()
                        w_pe(k.ready, q.ready, *readers)
                        pe.matmul(bank.tile, ident_h[:], tri0_q[:], start=True, stop=False)
                        for h in range(GROUP):
                            at = j * STRIP + b * P
                            m = pe.matmul(bank.tile[:, h * P:(h + 1) * P], q.tile[0:TROWS, h, b * P:(b + 1) * P],
                                          k.tile[0:TROWS, h, at:at + P], start=False, stop=(h == GROUP - 1))
                        w_dve(T(m), *mx_free)
                        m = V(dve.tensor_reduce(
                            mx.tile[:].rearrange("p (h b) s -> p h b s", b=BLOCKS)[:, :, b, 1],
                            bank.tile.rearrange("p (h n) -> p h n", h=GROUP), AX.X, ALU.max))
                        bank.readers.append(m)
                    return run

                if sparse:
                    steps += [tile_strided(h, b) for h in range(GROUP) for b in range(BLOCKS)]
                    steps += [tile_local(b) for b in range(BLOCKS)]
                    parts = 2
                else:
                    steps += [tile_dense(h, b, kc) for kc in range(j + 1) for h in range(GROUP) for b in range(BLOCKS)]
                    parts = j + 1

                def negate():
                    n3, n3_free = neg_parts.take()
                    w_dve((dve_done, dve_done.count), *n3_free)
                    m = V(dve.tensor_reduce(neg[:], mx.tile[:, :, 0:parts], AX.X, ALU.max, negate=True))
                    mx.readers.append(m)
                    w_dve(m)
                    w_dve(V(dve.tensor_copy(n3.tile[:, 0, :], neg[:])))
                    w_dve(V(dve.tensor_tensor(neg_rest[:], neg[:], n3.tile[:, 0, :], ALU.subtract)))
                    w_dve(V(dve.tensor_copy(n3.tile[:, 1, :], neg_rest[:])))
                    m = V(dve.tensor_tensor(n3.tile[:, 2, :], neg_rest[:], n3.tile[:, 1, :], ALU.subtract))
                    bank, readers = side_banks.take()
                    w_pe(m, *readers)
                    turned = bank.tile.bitcast(BF16)[0:3 * GROUP * BLOCKS, 0:P]
                    m = T(pe.transpose(turned, n3.tile[:].rearrange("p s n -> p (s n)"), ident_bf[:]))
                    n3.readers.append(m)
                    rows, rows_free = neg_rows.take()
                    w_dve(m, *rows_free)
                    m = V(dve.tensor_copy(rows.tile[:], turned))
                    bank.readers.append(m)
                    w_sp(m)
                    q.ready = q.load_signal.mark(sp.dma_start(
                        q.tile[TROWS:TROWS + MROWS, :, :].rearrange("s h (b p) -> s (h b) p", p=P), rows.tile[:]), 16)
                    rows.readers.append(q.ready)
                steps.append(negate)
                return steps

            def attend_steps(u):
                a, g, j = u
                k, v, sv = group_buffers[(a, g)]
                q = unit_state[u]
                pv, pv_free = pv_banks.take()
                steps, waiting = [], []
                tiles = [("strided", c) for c in range(NSTR // P)] + [("local", 0)] if sparse else \
                        [("dense", c) for c in range(BLOCKS * (j + 1))]

                def score(kind, c, pair, first_col):
                    slot, readers = score_pairs.take()
                    w_pe(q.ready, k.ready, *readers)
                    for i in range(2):
                        h = 2 * pair + i
                        o = slot.tile[:, i, first_col:STRIP]
                        if kind == "dense":
                            diagonal = c >= BLOCKS * j
                            m = pe.matmul(o, k.tile[:, h, c * P:(c + 1) * P], q.tile[:, h, first_col:STRIP],
                                          start=True, stop=not diagonal)
                            if diagonal:
                                m = pe.matmul(slot.tile[:, i, first_col:first_col + P], ident_bf[:], tri_key[:],
                                              start=False, stop=True)
                        elif kind == "strided":
                            ahead = j * STRIP - c * P * STRIDE
                            masked = ahead < P * STRIDE
                            m = pe.matmul(o, k.tile[:, h, c * P * STRIDE + STRIDE - 1:(c + 1) * P * STRIDE:STRIDE],
                                          q.tile[:, h, :], start=True, stop=not masked)
                            if masked:
                                at = max(ahead, -STRIP) + STRIP
                                m = pe.matmul(o, ident_h[:], mask_k[:, at:at + STRIP], start=False, stop=True)
                        else:
                            pe.matmul(o, ident_h[:], tri0_k[:], start=True, stop=False)
                            for b in range(BLOCKS):
                                at = j * STRIP + b * P
                                m = pe.matmul(slot.tile[:, i, b * P:(b + 1) * P], k.tile[:, h, at:at + P],
                                              q.tile[:, h, b * P:(b + 1) * P], start=False, stop=(b == BLOCKS - 1))
                    return slot, T(m)

                def exponent(slot, scored, first_col):
                    p, p_free = probs.take()
                    w_act(scored, *p_free)
                    p.ready = A(act.activation(p.tile[:, :, first_col:STRIP], slot.tile[:, :, first_col:STRIP],
                                               ACT.Exp, scale=SCALE))
                    slot.readers.append(p.ready)
                    return p

                def weigh(kind, c, pair_probs, first_col, first, last):
                    w_pe(v.ready, *[p.ready for p in pair_probs], *(pv_free if first else []))
                    if sparse:
                        w_pe(sv.ready)
                    for b in (range(BLOCKS) if kind == "local" else (None,)):
                        for h in range(GROUP):
                            probs_tile = pair_probs[h // 2].tile
                            rows = slice(h * GCOL, (h + 1) * GCOL)
                            if kind == "local":
                                cols = slice(b * P, (b + 1) * P)
                                vt = v.tile[:, BLOCKS * j + b, rows]
                            else:
                                cols = slice(first_col, STRIP)
                                vt = (sv if kind == "strided" else v).tile[:, c, rows]
                            m = pe.matmul(pv.tile[rows, cols], vt, probs_tile[:, h % 2, cols], start=first,
                                          stop=(last and b in (None, BLOCKS - 1)), skip_group_check=True)
                    m = T(m)
                    for p in pair_probs:
                        p.readers.append(m)
                    return m

                def tile_step(n, kind, c):
                    first_col = max(0, c - BLOCKS * j) * P if kind == "dense" else 0
                    held = []

                    def pair_run(pair):
                        def run():
                            slot, scored = score(kind, c, pair, first_col)
                            held.append(exponent(slot, scored, first_col))
                            if pair == 1:
                                waiting.append((kind, c, list(held), first_col, n == 0, n == len(tiles) - 1))
                                if len(waiting) > 1:
                                    weigh(*waiting.pop(0))
                        return run
                    return [pair_run(0), pair_run(1)]

                for n, (kind, c) in enumerate(tiles):
                    steps += tile_step(n, kind, c)

                def finish():
                    while waiting:
                        m = weigh(*waiting.pop(0))
                    q.readers.append(m)
                    if j == STRIPS - 1:
                        for s in (k, v) + ((sv,) if sparse else ()):
                            s.readers.append(m)
                    o, o_free = outs.take()
                    w_act(m, *o_free)
                    m = A(act.activation(o.tile[:], pv.tile, ACT.Copy))
                    pv.readers.append(m)
                    bank, readers = side_banks.take()
                    w_pe(m, *readers)
                    for b in range(BLOCKS):
                        m = pe.transpose(bank.tile[:, b * P:(b + 1) * P], o.tile[:, b * P:(b + 1) * P], ident[:])
                    m = T(m)
                    o.readers.append(m)
                    turned = bank.tile.rearrange("p (b h n) -> p b h n", b=BLOCKS, n=GCOL)
                    r, r_free = recips.take()
                    ao, ao_free = aos.take()
                    w_dve(m, *r_free, *ao_free)
                    w_dve(V(dve.reciprocal(r.tile[:], turned[:, :, :, HEAD_DIM])))
                    m = V(dve.tensor_tensor(
                        ao.tile[:].rearrange("p b (h n) -> p b h n", h=GROUP), turned[:, :, :, 0:HEAD_DIM],
                        r.tile[:].unsqueeze(3).broadcast_to([P, BLOCKS, GROUP, HEAD_DIM]), ALU.mult))
                    bank.readers.append(m)
                    r.readers.append(m)
                    w_sp(m)
                    cols = slice(g * GROUP * HEAD_DIM, (g + 1) * GROUP * HEAD_DIM)
                    ao.readers.append(ao.store_signal.mark(sp.dma_start(rows_of(ao_d[a], j)[:, :, cols], ao.tile[:]), 16))
                steps.append(finish)
                return steps

            load(units[0])
            load(units[1])
            for step in max_steps(units[0]):
                step()
            for n, u in enumerate(units):
                if n + 2 < len(units):
                    load(units[n + 2])
                side = max_steps(units[n + 1]) if n + 1 < len(units) else []
                spread(attend_steps(u), side, until=0.85)
        everyone_waits()

    attend((0,), "sparse")


    with ExitStack() as st3:
        weights = signal("middle_weights")
        wproj = sbuf(st3, "wproj0", [P, DC, DIM])
        wr = sbuf(st3, "w_rotary", [P, DC, 3 * DIM])
        wf = sbuf(st3, "w_moe_qkv", [P, DC, 3 * DIM])
        n1 = sbuf(st3, "n1", [P, DIM])
        qkw = sbuf(st3, "qk_norm_w", [P, 2, HEAD_DIM])
        cos = sbuf(st3, "cos", [P, TOKENS // P, HEAD_DIM])
        sin = sbuf(st3, "sin", [P, TOKENS // P, HEAD_DIM])
        for tile, src in ((wproj[:], d["L0_attn_c_proj_w"].rearrange("(c p) n -> p c n", p=P)),
                          (wr[:], d["L1_attn_Wqkv"].rearrange("(c p) n -> p c n", p=P)),
                          (wf[:, :, 0:DIM], d["L1_ffn_wq"].rearrange("(c p) n -> p c n", p=P)),
                          (wf[:, :, DIM:QK], d["L1_ffn_wk"].rearrange("(c p) n -> p c n", p=P)),
                          (wf[:, :, QK:3 * DIM], d["L1_ffn_wv"].rearrange("(c p) n -> p c n", p=P)),
                          (n1[:], d["L1_ffn_n1_w"].partition_broadcast(P)),
                          (qkw[:, 0, :], d["L1_ffn_qn_w"].partition_broadcast(P)),
                          (qkw[:, 1, :], d["L1_ffn_kn_w"].partition_broadcast(P)),
                          (cos[:], d["c_cos"]), (sin[:], d["c_sin"])):
            w_in = weights.mark(sp.dma_start(tile, src), 16)
        xs = ring(st3, "base_in", 2, [P, BLOCKS, DIM], loads=True, stores=True)
        aos = ring(st3, "ao_in", 2, [P, BLOCKS, DIM], loads=True)
        xns = ring(st3, "xn1_s", 2, [P, BLOCKS, DIM], stores=True)
        hs = ring(st3, "h_s", 1, [P, BLOCKS, DIM])
        xts = ring(st3, "t_s", 4, [P, DC, STRIP])
        qkns = ring(st3, "qkn1_s", 2, [P, BLOCKS, QK])
        ves = ring(st3, "ve1_s", 2, [P, BLOCKS, HEADS * GCOL], stores=True)
        stats = (sbuf(st3, "ln1_stats", [P, BLOCKS, 6]), sbuf(st3, "ln1_mv", [P, BLOCKS, 2]))
        small = sbuf(st3, "ln1_small", [P, 4, BLOCKS])
        ms = sbuf(st3, "ms1", [P, BLOCKS])
        junk = sbuf(st3, "junk1", [P, DIM])
        rot = sbuf(st3, "rot", [P, QK])
        turn = sbuf(st3, "turn", [P, QK])
        hsq = sbuf(st3, "head_squares", [P, QK])
        hms = sbuf(st3, "head_ms", [P, BLOCKS, 2 * HEADS])
        hsmall = sbuf(st3, "head_small", [P, 4, BLOCKS * 2 * HEADS])
        parts_ring = Ring([Slot(tuple(sbuf(st3, f"part1_{i}_{s}", [P, 4, STRIP], BF16) for s in range(3))
                                + (sbuf(st3, f"part1_{i}_r", [P, 4, STRIP]),), None, signal(f"parts1_stored{i}")) for i in range(1)])
        store_signals.extend(slot.store_signal for slot in parts_ring.slots)
        for slot in ves.slots:
            slot.ready = V(dve.memset(slot.tile[:], 1.0))
        quads = Ring([Slot(psum[:, 0:4, :], None)])
        qk_banks, v_banks, t_banks = bank_ring((4, 5)), bank_ring((6,)), bank_ring((7,))
        w_dve(w_in)
        w_pe(w_in)

        def load_mid(strip):
            got = []
            for r, src in ((xs, base_d), (aos, ao_d[0])):
                slot, readers = r.take()
                w_sp(*readers)
                slot.ready = slot.load_signal.mark(sp.dma_start(slot.tile[:], rows_of(src, strip)), 16)
                got.append(slot)
            return got

        def project_v(xt, w, tok, ve, b):
            bank, readers = v_banks.take()
            w_pe(*readers)
            for c in range(DC):
                m = pe.matmul(bank.tile[:, 0:DIM], xt[:, c, tok], w[:, c, QK:QK + DIM], start=(c == 0), stop=(c == DC - 1))
            m = T(m)
            w_act(m)
            m = A(act.activation(ve[:, b, :].rearrange("p (h n) -> p h n", n=GCOL)[:, :, 0:HEAD_DIM],
                                 bank.tile[:, 0:DIM].rearrange("p (h n) -> p h n", n=HEAD_DIM), ACT.Copy))
            bank.readers.append(m)
            return m

        nxt = load_mid(0)
        for strip in range(STRIPS):
            x, ao = nxt
            if strip + 1 < STRIPS:
                nxt = load_mid(strip + 1)
            aot, aot_free = xts.take()
            turned = to_features(ao.tile, ao.ready, t_banks, aot.tile, aot_free)
            ao.readers.append(turned)
            w_pe(turned)
            w_dve(x.ready)
            for b in range(BLOCKS):
                bank, readers = v_banks.take()
                w_pe(*readers)
                for c in range(DC):
                    m = pe.matmul(bank.tile[:, 0:DIM], aot.tile[:, c, b * P:(b + 1) * P], wproj[:, c, :],
                                  start=(c == 0), stop=(c == DC - 1))
                m_mm = T(m)
                w_dve(m_mm)
                m = V(dve.tensor_tensor(x.tile[:, b, :], x.tile[:, b, :], bank.tile[:, 0:DIM], ALU.add))
                bank.readers.append(m)
            aot.readers.append(m_mm)
            w_dve(m)
            w_sp(m)
            x.readers.append(x.store_signal.mark(sp.dma_start(rows_of(x1_d, strip), x.tile[:]), 16))
            xn, xn_free = xns.take()
            w_dve(*xn_free)
            normed = layer_norm(x.tile, xn.tile, stats, small)
            x.readers.append(normed)
            w_sp(normed)
            xn.readers.append(xn.store_signal.mark(sp.dma_start(rows_of(xn_d, strip), xn.tile[:]), 16))
            xt, xt_free = xts.take()
            turned = to_features(xn.tile, normed, t_banks, xt.tile, xt_free)
            h, h_free = hs.take()
            w_dve(normed)
            mean_square(xn.tile, junk, ms)
            rs, _ = norm_scale(small, ms[:], RMS_EPS)
            w_dve(*h_free)
            for b in range(BLOCKS):
                m = V(dve.scalar_tensor_tensor(out=h.tile[:, b, :], in0=xn.tile[:, b, :], scalar=rs[:, b:b + 1],
                                               in1=n1[:], op0=ALU.mult, op1=ALU.mult))
            xn.readers += [m, turned]
            ht, ht_free = xts.take()
            h_turned = to_features(h.tile, m, t_banks, ht.tile, ht_free)
            h.readers.append(h_turned)

            qkn, qkn_free = qkns.take()
            ve, ve_free = ves.take()
            w_pe(turned)
            w_dve(*qkn_free)
            w_act(*ve_free, ve.ready)
            for b in range(BLOCKS):
                tok = slice(b * P, (b + 1) * P)
                blk = strip * BLOCKS + b
                bank, readers = qk_banks.take()
                w_pe(*readers)
                for c in range(DC):
                    m = pe.matmul(bank.tile, xt.tile[:, c, tok], wr[:, c, 0:QK], start=(c == 0), stop=(c == DC - 1))
                w_dve(T(m), (dve_done, dve_done.count))
                sb4 = bank.tile.rearrange("p (h n two) -> p h n two", h=2 * HEADS, two=2)
                tr4 = turn[:].rearrange("p (h n two) -> p h n two", h=2 * HEADS, two=2)
                sn4 = sin[:, blk, :].rearrange("p (n two) -> p n two", two=2)
                for two in range(2):
                    V(dve.tensor_tensor(tr4[:, :, :, two], sb4[:, :, :, 1 - two],
                                        sn4[:, :, two].unsqueeze(1).broadcast_to([P, 2 * HEADS, HEAD_DIM // 2]), ALU.mult))
                m = V(dve.tensor_tensor(
                    rot[:].rearrange("p (h n) -> p h n", n=HEAD_DIM), bank.tile.rearrange("p (h n) -> p h n", n=HEAD_DIM),
                    cos[:, blk, :].unsqueeze(1).broadcast_to([P, 2 * HEADS, HEAD_DIM]), ALU.mult))
                bank.readers.append(m)
                w_dve(m)
                m_qk = V(dve.tensor_tensor(qkn.tile[:, b, :], rot[:], turn[:], ALU.add))
                m_v = project_v(xt.tile, wr, tok, ve.tile, b)
            xt.readers.append((pe_done, pe_done.count))
            ve.readers.append(store_v(1, strip, ve, m_v))
            quad, quad_readers = quads.take()
            parts, parts_free = parts_ring.take()
            rested, kept, m_t = make_parts(1, strip, qkn.tile, m_qk, quad.tile, quad_readers, parts, parts_free)
            quad.readers.append(rested)
            parts.readers.append(kept)
            qkn.readers.append(m_t)

            qkn, qkn_free = qkns.take()
            ve, ve_free = ves.take()
            w_pe(h_turned)
            w_dve(*qkn_free, (dve_done, dve_done.count))
            w_act(*ve_free, ve.ready)
            for b in range(BLOCKS):
                tok = slice(b * P, (b + 1) * P)
                bank, readers = qk_banks.take()
                w_pe(*readers)
                for c in range(DC):
                    m = pe.matmul(bank.tile, ht.tile[:, c, tok], wf[:, c, 0:QK], start=(c == 0), stop=(c == DC - 1))
                m = T(m)
                w_act(m, *qkn_free, (dve_done, dve_done.count))
                m = A(act.activation(qkn.tile[:, b, :], bank.tile, ACT.Copy))
                bank.readers.append(m)
                w_dve(m)
                w_dve(V(dve.tensor_tensor(hsq[:], qkn.tile[:, b, :], qkn.tile[:, b, :], ALU.mult)))
                w_dve(V(dve.tensor_reduce(hms[:, b, :], hsq[:].rearrange("p (h n) -> p h n", n=HEAD_DIM), AX.X, ALU.add)))
                m_v = project_v(ht.tile, wf, tok, ve.tile, b)
            ht.readers.append((pe_done, pe_done.count))
            ve.readers.append(store_v(2, strip, ve, m_v))
            hms_flat = hms[:].rearrange("p b h -> p (b h)")
            w_dve(V(dve.tensor_scalar(hms_flat, hms_flat, 1.0 / HEAD_DIM, None, ALU.mult)))
            rs, _ = norm_scale(hsmall, hms_flat, RMS_EPS)
            q3 = qkn.tile[:].rearrange("p b (h n) -> p (b h) n", n=HEAD_DIM)
            w_dve(V(dve.tensor_tensor(q3, q3, rs.unsqueeze(2).broadcast_to([P, BLOCKS * 2 * HEADS, HEAD_DIM]), ALU.mult)))
            for i in range(2):
                q4 = qkn.tile[:, :, i * DIM:(i + 1) * DIM].rearrange("p b (h n) -> p b h n", n=HEAD_DIM)
                for b in range(BLOCKS):
                    m_qk = V(dve.tensor_tensor(q4[:, b], q4[:, b],
                                               qkw[:, i, :].unsqueeze(1).broadcast_to([P, HEADS, HEAD_DIM]), ALU.mult))
            quad, quad_readers = quads.take()
            parts, parts_free = parts_ring.take()
            rested, kept, m_t = make_parts(2, strip, qkn.tile, m_qk, quad.tile, quad_readers, parts, parts_free)
            quad.readers.append(rested)
            parts.readers.append(kept)
            qkn.readers.append(m_t)
    everyone_waits()

    attend((1, 2), "dense")


    with ExitStack() as st5:
        weights = signal("finish_weights")

        def matrix(name, n_in, n_out):
            tile = sbuf(st5, f"w_{name}", [P, n_in // P, n_out])
            mark = weights.mark(sp.dma_start(tile[:], d[name].rearrange("(c p) n -> p c n", p=P)), 16)
            return tile, mark

        HID = 512
        wp, _ = matrix("L1_attn_Wproj", DIM, DIM)
        wo, _ = matrix("L1_ffn_wo", DIM, DIM)
        gate, _ = matrix("L1_ffn_gate_w", DIM, EXPERTS)
        e0u, _ = matrix("L1_ffn_e0_up", DIM, HID)
        e0d, _ = matrix("L1_ffn_e0_down", HID, DIM)
        e2a, _ = matrix("L1_ffn_e2_l1", DIM, HID)
        e2b, _ = matrix("L1_ffn_e2_l2", HID, HID)
        e2c, _ = matrix("L1_ffn_e2_l3", HID, HID)
        e2d, _ = matrix("L1_ffn_e2_l4", HID, DIM)
        e3a, _ = matrix("L1_ffn_e3_down", DIM, DIM)
        e3b, _ = matrix("L1_ffn_e3_up", DIM, HID)
        e3c, _ = matrix("L1_ffn_e3_out", HID, DIM)
        e1a, _ = matrix("L1_ffn_e1_w1", DIM, HID)
        e1b, _ = matrix("L1_ffn_e1_w2", DIM, HID)
        e1c, _ = matrix("L1_ffn_e1_down", HID, DIM)
        n2 = sbuf(st5, "n2", [P, DIM])
        lower = sbuf(st5, "lower", [P, EXPERTS, EXPERTS])
        weights.mark(sp.dma_start(n2[:], d["L1_ffn_n2_w"].partition_broadcast(P)), 16)
        w_in = weights.mark(sp.dma_start(lower[:], d["c_lower"]), 16)
        ao1s = ring(st5, "ao1_in", 1, [P, BLOCKS, DIM], loads=True)
        ao2s = ring(st5, "ao2_in", 1, [P, BLOCKS, DIM], loads=True)
        x1s = ring(st5, "x1_in", 2, [P, BLOCKS, DIM], loads=True)
        xas = ring(st5, "xa_in", 2, [P, BLOCKS, DIM], loads=True, stores=True)
        xfs = ring(st5, "xf", 1, [P, BLOCKS, DIM])
        xts = ring(st5, "t5_s", 4, [P, DC, STRIP])
        hids = ring(st5, "hid", 4, [P, HID // P, STRIP])
        small = sbuf(st5, "rms_small", [P, 4, BLOCKS])
        ms = sbuf(st5, "ms5", [P, BLOCKS])
        junk = sbuf(st5, "junk5", [P, DIM])
        logit = sbuf(st5, "logit", [P, BLOCKS, EXPERTS])
        prob = sbuf(st5, "prob", [P, BLOCKS, EXPERTS])
        red = sbuf(st5, "red", [P, BLOCKS, 4])
        beats = sbuf(st5, "beats", [P, BLOCKS, EXPERTS, EXPERTS])
        ties = sbuf(st5, "ties", [P, BLOCKS, EXPERTS, EXPERTS])
        rank = sbuf(st5, "rank", [P, BLOCKS, EXPERTS])
        wts = sbuf(st5, "wts", [P, BLOCKS, EXPERTS])
        t_banks, o_banks, h_banks = bank_ring((0, 1)), bank_ring((2, 3)), bank_ring((4, 5, 6, 7))
        w_dve(w_in)
        w_pe(w_in)

        def load_end(strip):
            got = []
            for r, src in ((ao1s, ao_d[1]), (ao2s, ao_d[2]), (x1s, x1_d), (xas, xn_d)):
                slot, readers = r.take()
                w_sp(*readers)
                slot.ready = slot.load_signal.mark(sp.dma_start(slot.tile[:], rows_of(src, strip)), 16)
                got.append(slot)
            return got

        def bcast(ap, n):
            return ap.unsqueeze(2).broadcast_to([P, BLOCKS, n])

        def hidden(src, src_ready, w, n_in, n_out, func):
            slot, free = hids.take()
            for f in range(n_out // P):
                bank, readers = h_banks.take()
                w_pe(src_ready, *readers)
                for c in range(n_in // P):
                    m = pe.matmul(bank.tile, w[:, c, f * P:(f + 1) * P], src[:, c, :], start=(c == 0), stop=(c == n_in // P - 1))
                w_act(T(m), *free)
                m = A(act.activation(slot.tile[:, f, :], bank.tile, func))
                bank.readers.append(m)
            return slot, m

        def expert_out(e, hid, ready, w, total, xa_ready):
            for b in range(BLOCKS):
                bank, readers = o_banks.take()
                w_pe(ready, *readers)
                for c in range(HID // P):
                    m = pe.matmul(bank.tile[:, 0:KEPT], hid.tile[:, c, b * P:(b + 1) * P], w[:, c, MASKED:DIM],
                                  start=(c == 0), stop=(c == HID // P - 1))
                m = T(m)
                w_dve(m, xa_ready)
                total_b = total[:, b, MASKED:DIM]
                m2 = V(dve.scalar_tensor_tensor(out=total_b, in0=bank.tile[:, 0:KEPT], scalar=wts[:, b, e:e + 1],
                                                in1=total_b, op0=ALU.mult, op1=ALU.add))
                bank.readers.append(m2)
            hid.readers.append(m)
            return m2

        nxt = load_end(0)
        for strip in range(STRIPS):
            ao1, ao2, x1, xa = nxt
            a1t, a1t_free = xts.take()
            t1 = to_features(ao1.tile, ao1.ready, t_banks, a1t.tile, a1t_free)
            ao1.readers.append(t1)
            a2t, a2t_free = xts.take()
            t2 = to_features(ao2.tile, ao2.ready, t_banks, a2t.tile, a2t_free)
            ao2.readers.append(t2)
            if strip + 1 < STRIPS:
                nxt = load_end(strip + 1)
            w_pe(t1, t2)
            w_dve(x1.ready, xa.ready)
            for b in range(BLOCKS):
                bank, readers = o_banks.take()
                w_pe(*readers)
                for c in range(DC):
                    m = pe.matmul(bank.tile[:, MASKED:DIM], a2t.tile[:, c, b * P:(b + 1) * P], wo[:, c, MASKED:DIM],
                                  start=(c == 0), stop=(c == DC - 1))
                m_mm = T(m)
                w_dve(m_mm)
                m = V(dve.tensor_tensor(xa.tile[:, b, MASKED:DIM], xa.tile[:, b, MASKED:DIM], bank.tile[:, MASKED:DIM], ALU.add))
                bank.readers.append(m)
            a2t.readers.append(m_mm)
            w_dve(m)
            mean_square(xa.tile, junk, ms)
            rs, _ = norm_scale(small, ms[:], RMS_EPS)
            xf, xf_free = xfs.take()
            w_dve(*xf_free)
            for b in range(BLOCKS):
                m = V(dve.scalar_tensor_tensor(out=xf.tile[:, b, :], in0=xa.tile[:, b, :], scalar=rs[:, b:b + 1],
                                               in1=n2[:], op0=ALU.mult, op1=ALU.mult))
            normed = m
            for b in range(BLOCKS):
                bank, readers = o_banks.take()
                w_pe(*readers)
                for c in range(DC):
                    m = pe.matmul(bank.tile[:, 0:DIM], a1t.tile[:, c, b * P:(b + 1) * P], wp[:, c, :],
                                  start=(c == 0), stop=(c == DC - 1))
                m_mm = T(m)
                w_dve(m_mm)
                m = V(dve.tensor_tensor(x1.tile[:, b, :], x1.tile[:, b, :], bank.tile[:, 0:DIM], ALU.add))
                bank.readers.append(m)
            a1t.readers.append(m_mm)
            w_dve(m)
            xft, xft_free = xts.take()
            xf_turned = to_features(xf.tile, normed, t_banks, xft.tile, xft_free)
            xf.readers.append(xf_turned)
            m_sum = V(dve.tensor_tensor(xa.tile[:], xa.tile[:], x1.tile[:], ALU.add))
            x1.readers.append(m_sum)

            bank, readers = o_banks.take()
            w_pe(xf_turned, *readers)
            for b in range(BLOCKS):
                for c in range(DC):
                    m = pe.matmul(bank.tile[:, b * EXPERTS:(b + 1) * EXPERTS], xft.tile[:, c, b * P:(b + 1) * P],
                                  gate[:, c, :], start=(c == 0), stop=(c == DC - 1))
            w_dve(T(m), (dve_done, dve_done.count))
            big = 3.4028234663852886e38
            m = V(dve.tensor_scalar(logit[:].rearrange("p b e -> p (b e)"), bank.tile[:, 0:BLOCKS * EXPERTS],
                                    big, -big, ALU.min, ALU.max))
            bank.readers.append(m)
            w_dve(m)
            w_dve(V(dve.tensor_reduce(red[:, :, 0], logit[:], AX.X, ALU.max)))
            m = V(dve.tensor_tensor(logit[:], logit[:], bcast(red[:, :, 0], EXPERTS), ALU.subtract))
            w_act(m)
            m = A(act.activation(prob[:], logit[:], ACT.Exp))
            w_dve(m)
            w_dve(V(dve.tensor_reduce(red[:, :, 1], prob[:], AX.X, ALU.add)))
            w_dve(V(dve.reciprocal(red[:, :, 2], red[:, :, 1])))
            w_dve(V(dve.tensor_tensor(prob[:], prob[:], bcast(red[:, :, 2], EXPERTS), ALU.mult)))
            other = prob[:].unsqueeze(2).broadcast_to([P, BLOCKS, EXPERTS, EXPERTS])
            own = prob[:].unsqueeze(3).broadcast_to([P, BLOCKS, EXPERTS, EXPERTS])
            for b in range(BLOCKS):
                V(dve.tensor_tensor(beats[:, b], other[:, b], own[:, b], ALU.is_gt))
                w_dve(V(dve.tensor_tensor(ties[:, b], other[:, b], own[:, b], ALU.is_equal)))
                m = V(dve.tensor_tensor(ties[:, b], ties[:, b], lower[:], ALU.mult))
            w_dve(m)
            w_dve(V(dve.tensor_tensor(beats[:].rearrange("p b e f -> p (b e f)"), beats[:].rearrange("p b e f -> p (b e f)"),
                                      ties[:].rearrange("p b e f -> p (b e f)"), ALU.add)))
            w_dve(V(dve.tensor_reduce(rank[:], beats[:], AX.X, ALU.add)))
            w_dve(V(dve.scalar_tensor_tensor(out=wts[:], in0=rank[:], scalar=1.5, in1=prob[:], op0=ALU.is_lt, op1=ALU.mult)))
            w_dve(V(dve.tensor_reduce(red[:, :, 0], wts[:], AX.X, ALU.add)))
            w_dve(V(dve.tensor_scalar(red[:, :, 0], red[:, :, 0], 1e-8, None, ALU.add)))
            w_dve(V(dve.reciprocal(red[:, :, 1], red[:, :, 0])))
            w_dve(V(dve.tensor_tensor(wts[:], wts[:], bcast(red[:, :, 1], EXPERTS), ALU.mult)))

            x_t = xft.tile
            h0, m0 = hidden(x_t, xf_turned, e0u, DIM, HID, ACT.Gelu)
            g1, mg1 = hidden(x_t, xf_turned, e2a, DIM, HID, ACT.Gelu)
            m = expert_out(0, h0, m0, e0d, xa.tile, m_sum)
            g2, mg2 = hidden(g1.tile, mg1, e2b, HID, HID, ACT.Gelu)
            g1.readers.append((pe_done, pe_done.count))
            r1, mr1 = hidden(x_t, xf_turned, e3a, DIM, DIM, ACT.Gelu)
            g3, mg3 = hidden(g2.tile, mg2, e2c, HID, HID, ACT.Gelu)
            g2.readers.append((pe_done, pe_done.count))
            r2, mr2 = hidden(r1.tile, mr1, e3b, DIM, HID, ACT.Gelu)
            r1.readers.append((pe_done, pe_done.count))
            w_dve(m)
            m = expert_out(2, g3, mg3, e2d, xa.tile, m)
            w_dve(m)
            s1, ms1 = hidden(x_t, xf_turned, e1a, DIM, HID, ACT.Silu)
            m = expert_out(3, r2, mr2, e3c, xa.tile, m)
            w_dve(m, ms1)
            for f in range(HID // P):
                bank, readers = h_banks.take()
                w_pe(*readers)
                for c in range(DC):
                    m1 = pe.matmul(bank.tile, e1b[:, c, f * P:(f + 1) * P], x_t[:, c, :], start=(c == 0), stop=(c == DC - 1))
                w_dve(T(m1))
                m1 = V(dve.tensor_tensor(s1.tile[:, f, :], s1.tile[:, f, :], bank.tile, ALU.mult))
                bank.readers.append(m1)
            xft.readers.append((pe_done, pe_done.count))
            m = expert_out(1, s1, m1, e1c, xa.tile, m)
            w_sp(m)
            xa.readers.append(xa.store_signal.mark(sp.dma_start(rows_of(out, strip), xa.tile[:]), 16))
    everyone_waits()


_TRANSPOSED = ("L1_ffn_wq", "L1_ffn_wk", "L1_ffn_wv", "L1_ffn_wo", "L1_ffn_gate_w", "L1_ffn_e0_up", "L1_ffn_e0_down",
               "L1_ffn_e1_w1", "L1_ffn_e1_w2", "L1_ffn_e1_down", "L1_ffn_e2_l1", "L1_ffn_e2_l2", "L1_ffn_e2_l3",
               "L1_ffn_e2_l4", "L1_ffn_e3_down", "L1_ffn_e3_up", "L1_ffn_e3_out")
_PLAIN = ("L0_attn_c_attn_w", "L0_attn_c_attn_b", "L0_attn_c_proj_w", "L0_attn_c_proj_b", "L0_ffn_kernel",
          "L0_ffn_input_scale", "L0_ffn_kernel_scale", "L0_ffn_bias", "L1_attn_Wqkv", "L1_attn_Wproj",
          "L1_ffn_n1_w", "L1_ffn_n2_w", "L1_ffn_qn_w", "L1_ffn_kn_w")


def shape_constants(bf16):
    part = np.arange(P)[:, None]
    col = np.arange(P)[None, :]
    key_after = (part > col)
    wide = np.arange((TOKENS - P) // STRIDE + NSTR)[None, :] - (TOKENS - P) // STRIDE
    ahead = np.arange(3 * STRIP)[None, :] - STRIP
    inv = (np.float32(1.0) / np.float32(10000.0) ** (np.arange(0, HEAD_DIM, 2, dtype=np.float32) / np.float32(HEAD_DIM)))
    angle = np.arange(TOKENS, dtype=np.float32)[:, None] * inv.astype(np.float32)[None, :]
    cos = np.repeat(np.cos(angle), 2, axis=-1).astype(np.float32)
    sin = np.repeat(np.sin(angle), 2, axis=-1).astype(np.float32)
    sin[:, 0::2] *= -1
    by_block = lambda t: np.ascontiguousarray(t.reshape(TOKENS // P, P, HEAD_DIM).transpose(1, 0, 2))
    lower = np.tile((np.arange(EXPERTS)[None, :] < np.arange(EXPERTS)[:, None])[None], (P, 1, 1))
    return {
        "c_ident": np.eye(P, dtype=np.float32),
        "c_ident_bf": np.eye(P, dtype=np.float32).astype(bf16),
        "c_ident_h": np.eye(P, dtype=np.float16),
        "c_tri_key": (key_after * np.float32(NEG1)).astype(bf16),
        "c_tri_query": (key_after.T * np.float32(NEG1)).astype(bf16),
        "c_tri0_k": np.tile(key_after * NEG0, (1, BLOCKS)).astype(np.float16),
        "c_tri0_q": np.tile(key_after.T * NEG0, (1, GROUP)).astype(np.float16),
        "c_mask_q": ((STRIDE * wide + STRIDE - 1 > part) * NEG0).astype(np.float16),
        "c_mask_k": ((STRIDE * part + STRIDE - 1 > ahead) * NEG0).astype(np.float16),
        "c_cos": by_block(cos), "c_sin": by_block(sin), "c_lower": lower.astype(np.float32),
    }


def kernel(**inputs):
    import concourse.bacc as _bacc
    from concourse import mybir as _mybir
    from concourse.bass_utils import run_bass_kernel_spmd as _run

    nc = _bacc.Bacc("TRN2", target_bir_lowering=False, num_devices=1)
    host = {"L0_attn_hidden_states": np.asarray(inputs["L0_attn_hidden_states"]).reshape(TOKENS, DIM)}
    for name in _PLAIN:
        host[name] = np.asarray(inputs[name])
    for name in _TRANSPOSED:
        host[name] = np.asarray(inputs[name]).T
    host.update(shape_constants(host["L0_ffn_kernel"].dtype))
    arrays, args = {}, {}
    for name, a in host.items():
        a = np.ascontiguousarray(a)
        arrays[f"in_{name}"] = a
        args[name] = nc.dram_tensor(f"in_{name}", a.shape, _mybir.dt.from_np(a.dtype), kind="ExternalInput").ap()
    out = nc.dram_tensor("out_dram", (TOKENS, DIM), F32, kind="ExternalOutput").ap()
    build(nc, args, out)
    r = _run(nc, [arrays], core_ids=[0])
    return r.results[0]["out_dram"].reshape(1, TOKENS, DIM)
```

```python
from contextlib import ExitStack

import numpy as np

import concourse.bass as bass
from concourse import mybir

F32 = mybir.dt.float32
BF16 = mybir.dt.bfloat16
F16 = mybir.dt.float16
U32 = mybir.dt.uint32
F32R = mybir.dt.float32r
ALU = mybir.AluOpType
ACT = mybir.ActivationFunctionType
AX = mybir.AxisListType

P = 128
TOKENS, DIM = 4096, 256
HEADS, HEAD_DIM = 16, 16
STRIP = 512
STRIPS = TOKENS // STRIP
BLOCKS = STRIP // P
DC = DIM // P
GROUP = 4
GROUPS = HEADS // GROUP
GCOL = 32
TERMS = ((0, 0), (0, 1), (1, 0), (1, 1), (0, 2), (2, 0))
TROWS = len(TERMS) * HEAD_DIM
MROWS = 3
SCALE = HEAD_DIM ** -0.5
STRIDE = 8
NSTR = TOKENS // STRIDE
NEG0 = -10000.0 / SCALE
NEG1 = -1e30
LN_EPS = 1e-5
RMS_EPS = 1.1920929e-07
MASKED = 64
KEPT = DIM - MASKED
QK = 2 * DIM
FP8_FIRST_NAN = 480.0
EXPERTS = 4


class Signal:

    def __init__(self, nc, ctx, name):
        self.sem, self.count = ctx.enter_context(nc.semaphore(name)), 0

    def mark(self, instruction, by=1):
        instruction.then_inc(self.sem, by)
        self.count += by
        return (self, self.count)


class Waiter:

    def __init__(self, engine):
        self.engine, self.seen = engine, {}

    def __call__(self, *marks):
        for mark in marks:
            if mark is None:
                continue
            signal, value = mark
            if self.seen.get(signal, 0) < value:
                self.engine.wait_ge(signal.sem, value)
                self.seen[signal] = value


class Slot:

    def __init__(self, tile, load_signal=None, store_signal=None):
        self.tile, self.load_signal, self.store_signal = tile, load_signal, store_signal
        self.readers, self.ready = [], None


class Ring:

    def __init__(self, slots):
        self.slots, self.at = slots, 0

    def take(self):
        slot = self.slots[self.at % len(self.slots)]
        self.at += 1
        old, slot.readers = slot.readers, []
        return slot, old


def build(nc, d, out):
    ctx = ExitStack()
    with ctx:
        _build(nc, ctx, d, out)


def _build(nc, ctx, d, out):
    pe, dve, act, pool, sp = nc.tensor, nc.vector, nc.scalar, nc.gpsimd, nc.sync
    w_pe, w_dve, w_act, w_pool, w_sp = (Waiter(e) for e in (pe, dve, act, pool, sp))

    def signal(name):
        return Signal(nc, ctx, name)

    def sbuf(stack, name, shape, dt=F32):
        return stack.enter_context(nc.sbuf_tensor(name, shape, dt))

    def ring(stack, name, n, shape, dt=F32, loads=False, stores=False):
        slots = [Slot(sbuf(stack, f"{name}{i}", shape, dt), signal(f"{name}{i}_loaded") if loads else None,
                      signal(f"{name}{i}_stored") if stores else None) for i in range(n)]
        store_signals.extend(slot.store_signal for slot in slots if stores)
        return Ring(slots)

    def scratch(name, shape, dt=F32):
        return nc.dram_tensor(name, shape, dt).ap()

    pe_done = signal("pe_done")
    dve_done = signal("dve_done")
    act_done = signal("act_done")
    pool_done = signal("pool_done")
    store_signals = []

    def V(instruction):
        return dve_done.mark(instruction)

    def A(instruction):
        return act_done.mark(instruction)

    def G(instruction):
        return pool_done.mark(instruction)

    def T(instruction):
        return pe_done.mark(instruction)

    base_d = scratch("base_scratch", (TOKENS, DIM))
    x1_d = scratch("x1_scratch", (TOKENS, DIM))
    xn_d = scratch("xn_scratch", (TOKENS, DIM))
    parts_d = [[scratch(f"parts_scratch{a}_{s}", (QK, TOKENS), BF16) for s in range(3)] for a in range(3)]
    v_d = [scratch(f"v_scratch{a}", (GROUPS, TOKENS, GROUP * GCOL)) for a in range(3)]
    ao_d = [scratch(f"ao_scratch{a}", (TOKENS, DIM)) for a in range(3)]

    psum = ctx.enter_context(nc.psum_tensor("psum", [P, 8, 512], F32))

    const_in = signal("const_in")
    ident = sbuf(ctx, "ident", [P, P])
    ident_bf = sbuf(ctx, "ident_bf", [P, P], BF16)
    ident_h = sbuf(ctx, "ident_h", [P, P], F16)
    tri_key = sbuf(ctx, "tri_key", [P, P], BF16)
    tri_query = sbuf(ctx, "tri_query", [P, P], BF16)
    for tile, name in ((ident, "c_ident"), (ident_bf, "c_ident_bf"), (ident_h, "c_ident_h"),
                       (tri_key, "c_tri_key"), (tri_query, "c_tri_query")):
        consts = const_in.mark(sp.dma_start(tile[:], d[name]), 16)

    def rows_of(dram, strip):
        return dram[strip * STRIP:(strip + 1) * STRIP, :].rearrange("(b p) n -> p b n", p=P)

    stored = {}


    def norm_scale(small, var, eps):
        ve, sd, rs, t = (small[:, i, :] for i in range(4))
        m = V(dve.tensor_scalar(ve, var, eps, None, ALU.add))
        w_act(m)
        m = A(act.activation(sd, ve, ACT.Sqrt))
        w_dve(m)
        w_dve(V(dve.reciprocal(rs, sd)))
        w_dve(V(dve.tensor_tensor(t, rs, rs, ALU.mult)))
        w_dve(V(dve.tensor_tensor(t, t, ve, ALU.mult)))
        w_dve(V(dve.tensor_scalar(t, t, -0.5, 1.5, ALU.mult, ALU.add)))
        m = V(dve.tensor_tensor(rs, rs, t, ALU.mult))
        w_dve(m)
        return rs, m

    def layer_norm(x, xn, stats, small):
        st, mv = stats
        for b in range(BLOCKS):
            m = V(dve.bn_stats(st[:, b, :], x[:, b, :]))
        w_dve(m)
        for b in range(BLOCKS):
            m = V(dve.bn_aggr(mv[:, b, :], st[:, b, :]))
        w_dve(m)
        rs, _ = norm_scale(small, mv[:, :, 1], LN_EPS)
        for b in range(BLOCKS):
            m = V(dve.tensor_scalar(xn[:, b, :], x[:, b, :], mv[:, b, 0:1], rs[:, b:b + 1],
                                    ALU.subtract, ALU.mult))
        return m

    def mean_square(x, junk, ms):
        for b in range(BLOCKS):
            m = V(dve.tensor_tensor_reduce(out=junk[:], in0=x[:, b, :], in1=x[:, b, :], scale=1.0 / DIM,
                                           scalar=0.0, op0=ALU.mult, op1=ALU.add, accum_out=ms[:, b:b + 1]))
            w_dve(m)
        return m

    def to_features(x, ready, pairs, xt, xt_free):
        bank, readers = pairs.take()
        w_pe(ready, *readers)
        for c in range(DC):
            for b in range(BLOCKS):
                m = pe.transpose(bank.tile[:, c, b * P:(b + 1) * P], x[:, b, c * P:(c + 1) * P], ident[:])
        turned = T(m)
        w_act(turned, *xt_free)
        m = A(act.activation(xt[:], bank.tile, ACT.Copy))
        bank.readers.append(m)
        return m, turned

    def to_split_features(x, ready, pairs, slot, free):
        high, low = slot.tile
        bank, readers = pairs.take()
        w_pe(ready, *readers)
        for c in range(DC):
            for b in range(BLOCKS):
                m = pe.transpose(bank.tile[:, c, b * P:(b + 1) * P], x[:, b, c * P:(c + 1) * P], ident[:])
        turned = T(m)
        w_act(turned, *free)
        m = A(act.activation(high[:], bank.tile, ACT.Copy))
        w_dve(m, *free)
        m = V(dve.tensor_tensor(low[:], bank.tile, high[:].bitcast(F32), ALU.subtract))
        bank.readers.append(m)
        return m, turned

    def split_ring(stack, name, n, shape):
        return Ring([Slot((sbuf(stack, f"{name}_high{i}", shape, F32R), sbuf(stack, f"{name}_low{i}", shape, F32R)))
                     for i in range(n)])

    def split_weight(stack, staging, name, src, n_in, cols):
        lo_col, hi_col = cols
        shape = [P, n_in // P, hi_col - lo_col]
        high, low = sbuf(stack, f"{name}_high", shape, F32R), sbuf(stack, f"{name}_low", shape, F32R)
        view = src.rearrange("(c p) n -> p c n", p=P)
        for c in range(n_in // P):
            slot, readers = staging.take()
            w_sp(*readers)
            part = slot.tile[:, 0:shape[2]]
            w_dve(slot.load_signal.mark(sp.dma_start(part, view[:, c, lo_col:hi_col]), 16))
            w_dve(V(dve.tensor_copy(high[:, c, :], part)))
            m = V(dve.tensor_tensor(low[:, c, :], part, high[:, c, :].bitcast(F32), ALU.subtract))
            slot.readers.append(m)
        return (high, low), m

    def split_by_pool(staging, src, high, low):
        view = src.rearrange("(c p) n -> p c n", p=P)

        def chunk(c):
            slot, readers = staging.take()
            w_sp(*readers)
            part = slot.tile[:, 0:high.shape[2]]
            w_pool(slot.load_signal.mark(sp.dma_start(part, view[:, c, :]), 16))
            w_pool(G(pool.tensor_copy(high[:, c, :], part)))
            m = G(pool.tensor_tensor(low[:, c, :], part, high[:, c, :].bitcast(F32), ALU.subtract))
            slot.readers.append(m)
            return m
        return [lambda c=c: chunk(c) for c in range(high.shape[1])]

    def product(out_ap, left, right, chunks):
        pairs = [(l, r, c) for c in range(chunks) for l, r in ((0, 0), (0, 1), (1, 0))]
        for n, (l, r, c) in enumerate(pairs):
            m = pe.matmul(out_ap, left(l, c), right(r, c), start=(n == 0), stop=(n == len(pairs) - 1))
        return m

    def bank_ring(ids):
        return Ring([Slot(psum[:, i, :], None) for i in ids])

    def pair_ring(ids):
        return Ring([Slot(psum[:, i:i + 2, :]) for i in ids])

    def make_parts(a, strip, qkn, ready, pairs, parts_slot, parts_free, bias=None):
        p1, p2, p3, rest = parts_slot.tile
        rests = []
        for half in range(2):
            bank, readers = pairs.take()
            fs = slice(2 * half, 2 * half + 2)
            w_pe(ready, *readers)
            for i in range(2):
                f = 2 * half + i
                for b in range(BLOCKS):
                    m = pe.transpose(bank.tile[:, i, b * P:(b + 1) * P], qkn[:, b, f * P:(f + 1) * P], ident[:])
            turned = T(m)
            w_act(turned, *parts_free)
            if bias is None:
                first = A(act.activation(p1[:, fs, :], bank.tile, ACT.Copy))
                w_dve(first)
                rested = V(dve.tensor_tensor(rest[:, fs, :], bank.tile, p1[:, fs, :], ALU.subtract))
            else:
                for i in range(2):
                    f = 2 * half + i
                    first = A(act.activation(p1[:, f, :], bank.tile[:, i, :], ACT.Identity, bias=bias[:, f:f + 1]))
                    w_dve(first)
                    rested = V(dve.scalar_tensor_tensor(out=rest[:, f, :], in0=bank.tile[:, i, :], scalar=bias[:, f:f + 1],
                                                        in1=p1[:, f, :], op0=ALU.add, op1=ALU.subtract))
            bank.readers.append(rested)
            rests.append(rested)
        for half, rested in enumerate(rests):
            fs = slice(2 * half, 2 * half + 2)
            w_act(rested)
            second = A(act.activation(p2[:, fs, :], rest[:, fs, :], ACT.Copy))
            w_pool(second, *parts_free)
            third = G(pool.tensor_tensor(p3[:, fs, :], rest[:, fs, :], p2[:, fs, :], ALU.subtract))
        w_sp(first, third)
        for s, part in enumerate((p1, p2, p3)):
            dst = parts_d[a][s][:, strip * STRIP:(strip + 1) * STRIP].rearrange("(m p) t -> p m t", p=P)
            kept = parts_slot.store_signal.mark(sp.dma_start(dst, part[:]), 16)
        return turned, kept

    def parts_buffers(stack, name, n):
        slots = [Slot(tuple(sbuf(stack, f"{name}{i}_{s}", [P, QK // P, STRIP], BF16) for s in range(3))
                      + (sbuf(stack, f"{name}{i}_rest", [P, QK // P, STRIP]),), None, signal(f"{name}{i}_stored")) for i in range(n)]
        store_signals.extend(slot.store_signal for slot in slots)
        return Ring(slots)

    def store_v(a, strip, ve_slot, ready):
        w_sp(ready)
        for g in range(GROUPS):
            dst = v_d[a][g, strip * STRIP:(strip + 1) * STRIP, :].rearrange("(b p) n -> p b n", p=P)
            kept = ve_slot.store_signal.mark(sp.dma_start(dst, ve_slot.tile[:, :, g * GROUP * GCOL:(g + 1) * GROUP * GCOL]), 16)
        return kept

    def v_columns(ve, b, n=1):
        return ve[:, b:b + n, :].rearrange("p b (h n) -> p b h n", n=GCOL)[:, :, :, 0:HEAD_DIM]

    def everyone_waits():
        last = [(s, s.count) for s in [pe_done, dve_done, act_done, pool_done] + store_signals if s.count]
        for w in (w_pe, w_dve, w_act, w_pool, w_sp):
            w(*last)

    w = {}

    def matrix(stack, staging, name, src, n_in, n_out, first=0):
        shape = [P, n_in // P, n_out - first]
        high, low = sbuf(stack, name + "_high", shape, F32R), sbuf(stack, name + "_low", shape, F32R)
        w[name] = (high, low)

        def step(split):
            w[name + "_ready"] = split()
        return [lambda split=split: step(split)
                for split in split_by_pool(staging, src[:, first:n_out], high, low)]


    with ExitStack() as st1:
        weights = signal("embed_weights")
        staging = ring(st1, "stage1_", 2, [P, 3 * DIM], loads=True)
        bqkv = sbuf(st1, "bqkv0", [P, 3 * DIM])
        bqk_t = sbuf(st1, "bqk_t", [P, QK // P])
        bproj = sbuf(st1, "bproj0", [P, DIM])
        kraw = sbuf(st1, "fp8_w_raw", [P, DC, DIM], BF16)
        bias8 = sbuf(st1, "fp8_bias", [P, DIM], BF16)
        scales = sbuf(st1, "fp8_scales", [P, 2])
        xs = ring(st1, "x_in", 3, [P, BLOCKS, DIM], loads=True, stores=True)

        def load_x(strip):
            slot, readers = xs.take()
            w_sp(*readers)
            slot.ready = slot.load_signal.mark(sp.dma_start(slot.tile[:], rows_of(d["L0_attn_hidden_states"], strip)), 16)
            return slot

        x_slots = [load_x(0)]
        for tile, src in ((bqkv[:], d["L0_attn_c_attn_b"].partition_broadcast(P)),
                          (bqk_t[:], d["bias_by_feature"]),
                          (bproj[:], d["L0_attn_c_proj_b"].partition_broadcast(P)),
                          (kraw[:], d["L0_ffn_kernel"].rearrange("(c p) n -> p c n", p=P)),
                          (bias8[:], d["L0_ffn_bias"].partition_broadcast(P)),
                          (scales[:, 0:1], d["L0_ffn_input_scale"].partition_broadcast(P)),
                          (scales[:, 1:2], d["L0_ffn_kernel_scale"].partition_broadcast(P))):
            w_in = weights.mark(sp.dma_start(tile, src), 16)

        recip = sbuf(st1, "fp8_recip", [P, 2])
        product8 = sbuf(st1, "fp8_product", [P, 1])
        q8_a = sbuf(st1, "q8_a", [P, DC, STRIP])
        q8_b = sbuf(st1, "q8_b", [P, DC, STRIP])
        q8_c = sbuf(st1, "q8_c", [P, DC, STRIP])
        q8_x = sbuf(st1, "q8_x", [P, DC, STRIP], BF16)

        def round_fp8(src, scale_column, width, out_tile, free):
            a, b, c = (t[:, :, 0:width] for t in (q8_a, q8_b, q8_c))
            w_dve(V(dve.tensor_scalar(a, src, recip[:, scale_column:scale_column + 1], None, ALU.mult)))
            w_dve(V(dve.tensor_scalar(b.bitcast(U32), a.bitcast(U32), 0x7F800000, None, ALU.bitwise_and)))
            w_dve(V(dve.tensor_scalar(b, b, 2.0 ** -6, 1.5 * 2.0 ** 20, ALU.max, ALU.mult)))
            w_dve(V(dve.tensor_tensor(a, a, b, ALU.add)))
            rounded = V(dve.tensor_tensor(a, a, b, ALU.subtract))

            def square():
                w_act(rounded)
                w_dve(A(act.activation(c, a, ACT.Square)))

            def find_nans():
                w_act(V(dve.tensor_scalar(c, c, FP8_FIRST_NAN ** 2, 3e38, ALU.is_ge, ALU.mult)))
                w_dve(A(act.activation(c, c, ACT.Square)), *free)

            def write():
                return V(dve.scalar_tensor_tensor(out=out_tile, in0=c, scalar=0.0, in1=a, op0=ALU.mult, op1=ALU.add))
            return square, find_nans, write

        xns = ring(st1, "xn_s", 2, [P, BLOCKS, DIM])
        xts = split_ring(st1, "xt", 2, [P, DC, STRIP])
        xqs = ring(st1, "xq_s", 2, [P, DC, STRIP], BF16)
        qkns = ring(st1, "qkn_s", 2, [P, BLOCKS, QK])
        ves = ring(st1, "ve_s", 2, [P, BLOCKS, HEADS * GCOL], stores=True)
        ys = ring(st1, "y_s", 2, [P, 2, DIM], BF16)
        stats = (sbuf(st1, "ln_stats", [P, BLOCKS, 6]), sbuf(st1, "ln_mv", [P, BLOCKS, 2]))
        small = sbuf(st1, "ln_small", [P, 4, BLOCKS])
        parts_ring = parts_buffers(st1, "part_", 1)
        for slot in ves.slots:
            slot.ready = G(pool.memset(slot.tile[:], 1.0))
        w_dve(*[slot.ready for slot in ves.slots])
        pairs, qk_banks, v_banks = pair_ring((0, 2)), bank_ring((4, 5)), bank_ring((6, 7))
        state = {}

        def norm(strip):
            if strip + 1 < STRIPS:
                x_slots.append(load_x(strip + 1))
            x = x_slots[strip]
            xn, xn_free = xns.take()
            w_dve(x.ready, *xn_free)
            state[strip] = dict(x=x, xn=xn, normed=layer_norm(x.tile, xn.tile, stats, small))

        def turn(strip):
            st = state[strip]
            xt, xt_free = xts.take()
            st["xt_ready"], read = to_split_features(st["xn"].tile, st["normed"], pairs, xt, xt_free)
            st["xt"] = xt
            st["xn"].readers.append(read)
            x = st["x"]
            w_pool(st["normed"])
            for b in range(BLOCKS):
                st["based"] = G(pool.tensor_tensor(x.tile[:, b, :], x.tile[:, b, :], bproj[:], ALU.add))

        def quantise(strip):
            st = state[strip]
            xq, xq_free = xqs.take()
            w_dve(*state.pop("q8_free"), st["xt_ready"])
            high, low = st["xt"].tile
            m_x = V(dve.tensor_tensor(q8_x[:], high[:].bitcast(F32), low[:].bitcast(F32), ALU.add))
            w_dve(m_x)
            st["fp8_steps"] = round_fp8(q8_x[:], 0, STRIP, xq.tile[:], xq_free)
            st["xq"] = xq
            st["xt"].readers.append(m_x)

        def qkv(strip):
            st = state[strip]
            high_low = st["xt"].tile
            square, find_nans, write = st["fp8_steps"]
            qkn, qkn_free = qkns.take()
            ve, ve_free = ves.take()
            w_pe(st["xt_ready"], m_w)
            w_act(*qkn_free)
            w_dve(*ve_free)
            for b in range(BLOCKS):
                tok = slice(b * P, (b + 1) * P)
                bank, readers = qk_banks.take()
                w_pe(*readers)
                w_act(T(product(bank.tile, lambda l, c: high_low[l][:, c, tok], lambda r, c: wqkv[r][:, c, 0:QK], DC)))
                m_qk = A(act.activation(qkn.tile[:, b, :], bank.tile, ACT.Copy))
                bank.readers.append(m_qk)
                if b % 2 == 0:
                    vbank, readers = v_banks.take()
                    w_pe(*readers)
                m_mm = T(product(vbank.tile[:, b % 2 * DIM:(b % 2 + 1) * DIM], lambda l, c: high_low[l][:, c, tok],
                                 lambda r, c: wqkv[r][:, c, QK:QK + DIM], DC))
                if b % 2 == 1:
                    w_dve(m_mm)
                    for i in (b - 1, b):
                        m_v = V(dve.tensor_tensor(
                            v_columns(ve.tile, i)[:, 0], vbank.tile[:, i % 2 * DIM:(i % 2 + 1) * DIM].rearrange("p (h n) -> p h n", n=HEAD_DIM),
                            bqkv[:, QK:QK + DIM].rearrange("p (h n) -> p h n", n=HEAD_DIM), ALU.add))
                    vbank.readers.append(m_v)
                if b == 1:
                    square()
                    if strip + 1 < STRIPS:
                        norm(strip + 1)
                if b == 2:
                    find_nans()
            st["xq_ready"] = write()
            state["q8_free"] = [st["xq_ready"]]
            st["xt"].readers.append(m_mm)
            ve.readers.append(store_v(0, strip, ve, m_v))
            st["qkn"], st["qk_ready"] = qkn, m_qk

        def parts(strip):
            st = state[strip]
            slot, parts_free = parts_ring.take()
            turned, kept = make_parts(0, strip, st["qkn"].tile, st["qk_ready"], pairs, slot, parts_free, bias=bqk_t)
            slot.readers.append(kept)
            st["qkn"].readers.append(turned)

        def gemm8(strip):
            st = state[strip]
            x = st["x"]
            w_pe(st["xq_ready"], m_kq)
            for half in range(BLOCKS // 2):
                bank, readers = v_banks.take()
                w_pe(*readers)
                for b in (2 * half, 2 * half + 1):
                    for c in range(DC):
                        m = pe.matmul(bank.tile[:, b % 2 * DIM:(b % 2 + 1) * DIM], st["xq"].tile[:, c, b * P:(b + 1) * P],
                                      kq[:, c, :], start=(c == 0), stop=(c == DC - 1))
                m_mm = T(m)
                y, y_free = ys.take()
                w_act(m_mm, *y_free)
                m = A(act.activation(y.tile[:].rearrange("p b n -> p (b n)"), bank.tile, ACT.Copy, scale=product8[:, 0:1]))
                bank.readers.append(m)
                w_dve(m, st["based"])
                w_dve(V(dve.tensor_tensor(y.tile[:], y.tile[:], bias8[:].unsqueeze(1).broadcast_to([P, 2, DIM]), ALU.add)))
                x_half = x.tile[:, 2 * half:2 * half + 2, :]
                m = V(dve.tensor_tensor(x_half, x_half, y.tile[:], ALU.add))
                y.readers.append(m)
            st["xq"].readers.append(m_mm)
            w_sp(m)
            x.readers.append(x.store_signal.mark(sp.dma_start(rows_of(base_d, strip), x.tile[:]), 16))

        w_pe(consts)
        norm(0)
        w_pool(w_in)
        turn(0)
        w_act(w_in)
        w_dve(w_in)
        wqkv, m_w = split_weight(st1, staging, "wqkv0", d["L0_attn_c_attn_w"], DIM, (0, 3 * DIM))
        V(dve.reciprocal(recip[:], scales[:]))
        w_dve(V(dve.tensor_tensor(product8[:], scales[:, 0:1], scales[:, 1:2], ALU.mult)))
        kq = sbuf(st1, "fp8_w", [P, DC, DIM], BF16)
        square, find_nans, write = round_fp8(kraw[:], 1, DIM, kq[:], [])
        square()
        find_nans()
        m_kq = write()
        state["q8_free"] = [m_kq]
        quantise(0)
        for strip in range(STRIPS):
            more = strip + 1 < STRIPS
            qkv(strip)
            parts(strip)
            if more:
                turn(strip + 1)
            gemm8(strip)
            if more:
                quantise(strip + 1)
    everyone_waits()


    def attend(jobs, stage, beside=()):
        groups = [(a, g) for a in jobs for g in range(GROUPS)]
        units = [(a, g, j if n % 2 == 0 else STRIPS - 1 - j) for n, (a, g) in enumerate(groups) for j in range(STRIPS)]
        sparse = jobs == (0,)
        with ExitStack() as st:
            keys = ring(st, f"keys_{stage}_", 2, [TROWS + MROWS, GROUP, TOKENS], BF16, loads=True)
            values = ring(st, f"values_{stage}_", 2, [P, TOKENS // P, GROUP * GCOL], loads=True)
            queries = ring(st, f"queries_{stage}_", 8, [TROWS + MROWS, GROUP, STRIP], BF16, loads=True)
            probs = ring(st, f"probs_{stage}_", 6, [P, 2, STRIP])
            maxes = ring(st, f"maxes_{stage}_", 3, [P, GROUP * BLOCKS, STRIPS])
            neg = sbuf(st, f"neg_{stage}", [P, GROUP * BLOCKS])
            neg_rest = sbuf(st, f"neg_rest_{stage}", [P, GROUP * BLOCKS])
            neg_parts = ring(st, f"neg_parts_{stage}_", 2, [P, 3, GROUP * BLOCKS], BF16)
            neg_rows = ring(st, f"neg_rows_{stage}_", 2, [3 * GROUP * BLOCKS, P], BF16)
            outs = ring(st, f"outs_{stage}_", 2, [P, STRIP])
            recips = ring(st, f"recips_{stage}_", 2, [P, BLOCKS, GROUP])
            aos = ring(st, f"aos_{stage}_", 2, [P, BLOCKS, GROUP * HEAD_DIM], stores=True)
            mask_signal = signal(f"masks_{stage}")
            if sparse:
                str_values = ring(st, "str_values_", 2, [P, NSTR // P, GROUP * GCOL], loads=True)
                mask_q = sbuf(st, "mask_q", [P, P // STRIDE], F16)
                mask_k = sbuf(st, "mask_k", [P, 2 * P * STRIDE - STRIP], F16)
                after_bias = sbuf(st, "after_bias", [P, 1])
                w_act(V(dve.memset(after_bias[:], NEG0 * SCALE)))
                tri0_q = sbuf(st, "tri0_q", [P, STRIP], F16)
                tri0_k = sbuf(st, "tri0_k", [P, STRIP], F16)
                for tile, name in ((mask_q, "c_mask_q"), (mask_k, "c_mask_k"), (tri0_q, "c_tri0_q"), (tri0_k, "c_tri0_k")):
                    masks = mask_signal.mark(sp.dma_start(tile[:], d[name]), 16)
            for slot in keys.slots:
                masks = mask_signal.mark(sp.dma_start(slot.tile[TROWS:TROWS + MROWS, :, :], d["c_ones"]), 16)
            w_pe(masks)
            score_pairs = Ring([Slot(psum[:, 0:2, :], None), Slot(psum[:, 2:4, :], None)])
            pv_banks, side_banks = bank_ring((4,)), bank_ring((5, 6, 7))
            group_buffers, unit_state = {}, {}

            first_keys = signal(f"first_keys_{stage}")

            def load_keys(u, tokens=slice(0, TOKENS)):
                a, g, _ = u
                if tokens.start == 0:
                    k, k_readers = keys.take()
                    w_sp(*k_readers)
                    group_buffers[(a, g)] = [k, None, None]
                k = group_buffers[(a, g)][0]
                loaded = first_keys if tokens.stop < TOKENS else k.load_signal
                for n, (_, part) in enumerate(TERMS):
                    src = parts_d[a][part][DIM + g * GROUP * HEAD_DIM:DIM + (g + 1) * GROUP * HEAD_DIM, tokens]
                    k.ready = loaded.mark(sp.dma_start(
                        k.tile[n * HEAD_DIM:(n + 1) * HEAD_DIM, :, tokens],
                        src.rearrange("(h e) t -> e h t", e=HEAD_DIM)), 16)

            def keys_ready(k, u):
                return (first_keys, first_keys.count) if u == units[0] and not sparse else k.ready

            def load_values(u):
                a, g, _ = u
                v, v_readers = values.take()
                w_sp(*v_readers)
                v.ready = v.load_signal.mark(sp.dma_start(
                    v.tile[:], v_d[a][g].rearrange("(b p) n -> p b n", p=P)), 16)
                sv = None
                if sparse:
                    sv, sv_readers = str_values.take()
                    w_sp(*sv_readers)
                    sv.ready = sv.load_signal.mark(sp.dma_start(
                        sv.tile[:], v_d[a][g].rearrange("(c p e) n -> p c e n", p=P, e=STRIDE)[:, :, STRIDE - 1, :]), 16)
                group_buffers[(a, g)][1:] = [v, sv]

            def load_queries(u):
                a, g, j = u
                q, q_readers = queries.take()
                w_sp(*q_readers)
                for n, (part, _) in enumerate(TERMS):
                    src = parts_d[a][part][g * GROUP * HEAD_DIM:(g + 1) * GROUP * HEAD_DIM, j * STRIP:(j + 1) * STRIP]
                    q.ready = q.load_signal.mark(sp.dma_start(
                        q.tile[n * HEAD_DIM:(n + 1) * HEAD_DIM, :, :],
                        src.rearrange("(h e) t -> e h t", e=HEAD_DIM)), 16)
                unit_state[u] = q

            def max_steps(u):
                a, g, j = u
                steps, now = [], {}

                def begin():
                    now["k"], now["q"] = group_buffers[(a, g)][0], unit_state[u]
                    now["mx"], now["mx_free"] = maxes.take()

                def current():
                    if not now:
                        begin()
                    return now["k"], now["q"], now["mx"], now["mx_free"]

                def tile_dense(h, b, kc):
                    def run():
                        k, q, mx, mx_free = current()
                        bank, readers = side_banks.take()
                        w_pe(keys_ready(k, u), q.ready, *readers)
                        diagonal = kc == j
                        width = (b + 1) * P if diagonal else STRIP
                        m = pe.matmul(bank.tile[:, 0:width], q.tile[0:TROWS, h, b * P:(b + 1) * P],
                                      k.tile[0:TROWS, h, kc * STRIP:kc * STRIP + width], start=True, stop=not diagonal)
                        if diagonal:
                            m = pe.matmul(bank.tile[:, b * P:(b + 1) * P], ident_bf[:], tri_query[:], start=False, stop=True)
                        w_dve(T(m), *mx_free)
                        m = V(dve.tensor_reduce(mx.tile[:, h * BLOCKS + b, kc:kc + 1], bank.tile[:, 0:width], AX.X, ALU.max))
                        bank.readers.append(m)
                    return run

                def tile_strided(h, b):
                    def run():
                        k, q, mx, mx_free = current()
                        bank, readers = side_banks.take()
                        w_pe(keys_ready(k, u), q.ready, *readers)
                        pe.matmul(bank.tile, q.tile[0:TROWS, h, b * P:(b + 1) * P],
                                  k.tile[0:TROWS, h, STRIDE - 1::STRIDE], start=True, stop=False)
                        own = (BLOCKS * j + b) * P // STRIDE
                        after = own + P // STRIDE
                        m = pe.matmul(bank.tile[:, own:after], ident_h[:], mask_q[:], start=False, stop=True)
                        w_dve(T(m), *mx_free)
                        m = V(dve.tensor_reduce(mx.tile[:, h * BLOCKS + b, 0:1], bank.tile[:, 0:after], AX.X, ALU.max))
                        if after < NSTR:
                            m = V(dve.tensor_reduce(mx.tile[:, h * BLOCKS + b, 2:3], bank.tile[:, after:NSTR], AX.X, ALU.max))
                        elif h == 0:
                            m = V(dve.memset(mx.tile[:, b::BLOCKS, 2], -3e38))
                        bank.readers.append(m)
                    return run

                def tile_local(b):
                    def run():
                        k, q, mx, mx_free = current()
                        bank, readers = side_banks.take()
                        w_pe(keys_ready(k, u), q.ready, *readers)
                        pe.matmul(bank.tile, ident_h[:], tri0_q[:], start=True, stop=False)
                        for h in range(GROUP):
                            at = j * STRIP + b * P
                            m = pe.matmul(bank.tile[:, h * P:(h + 1) * P], q.tile[0:TROWS, h, b * P:(b + 1) * P],
                                          k.tile[0:TROWS, h, at:at + P], start=False, stop=(h == GROUP - 1))
                        w_dve(T(m), *mx_free)
                        m = V(dve.tensor_reduce(
                            mx.tile[:].rearrange("p (h b) s -> p h b s", b=BLOCKS)[:, :, b, 1],
                            bank.tile.rearrange("p (h n) -> p h n", h=GROUP), AX.X, ALU.max))
                        bank.readers.append(m)
                    return run

                if sparse:
                    steps += [tile_strided(h, b) for h in range(GROUP) for b in range(BLOCKS)]
                    steps += [tile_local(b) for b in range(BLOCKS)]
                    parts = 3
                else:
                    steps += [tile_dense(h, b, kc) for kc in range(j + 1) for h in range(GROUP) for b in range(BLOCKS)]
                    parts = j + 1

                handed = []

                def negate():
                    mx = now["mx"]
                    n3, n3_free = neg_parts.take()
                    w_dve((dve_done, dve_done.count), *n3_free)
                    if sparse:
                        w_dve(V(dve.tensor_scalar(mx.tile[:, :, 2], mx.tile[:, :, 2], NEG0, None, ALU.add)))
                    m = V(dve.tensor_reduce(neg[:], mx.tile[:, :, 0:parts], AX.X, ALU.max, negate=True))
                    mx.readers.append(m)
                    w_dve(m)
                    w_dve(V(dve.tensor_copy(n3.tile[:, 0, :], neg[:])))
                    w_dve(V(dve.tensor_tensor(neg_rest[:], neg[:], n3.tile[:, 0, :], ALU.subtract)))
                    w_dve(V(dve.tensor_copy(n3.tile[:, 1, :], neg_rest[:])))
                    m = V(dve.tensor_tensor(n3.tile[:, 2, :], neg_rest[:], n3.tile[:, 1, :], ALU.subtract))
                    handed.append((n3, m))

                def hand_over():
                    q = now["q"]
                    n3, m = handed[0]
                    bank, readers = side_banks.take()
                    w_pe(m, *readers)
                    turned = bank.tile.bitcast(BF16)[0:3 * GROUP * BLOCKS, 0:P]
                    m = T(pe.transpose(turned, n3.tile[:].rearrange("p s n -> p (s n)"), ident_bf[:]))
                    n3.readers.append(m)
                    rows, rows_free = neg_rows.take()
                    w_dve(m, *rows_free)
                    m = V(dve.tensor_copy(rows.tile[:], turned))
                    bank.readers.append(m)
                    w_sp(m)
                    q.ready = q.load_signal.mark(sp.dma_start(
                        q.tile[TROWS:TROWS + MROWS, :, :].rearrange("s h (b p) -> s (h b) p", p=P), rows.tile[:]), 16)
                    rows.readers.append(q.ready)
                steps.append(negate)
                return steps, hand_over

            def attend_steps(u):
                a, g, j = u
                k, v, sv = group_buffers[(a, g)]
                q = unit_state[u]
                pv, pv_free = pv_banks.take()
                steps, waiting = [], []
                tiles = [("strided", c) for c in range(NSTR // P)] + [("local", 0)] if sparse else \
                        [("dense", c) for c in range(BLOCKS * (j + 1))]

                def score(kind, c, slot, h, first_col):
                    i = h % 2
                    o = slot.tile[:, i, first_col:STRIP]
                    if kind == "dense":
                        diagonal = c >= BLOCKS * j
                        m = pe.matmul(o, k.tile[:, h, c * P:(c + 1) * P], q.tile[:, h, first_col:STRIP],
                                      start=True, stop=not diagonal)
                        if diagonal:
                            m = pe.matmul(slot.tile[:, i, first_col:first_col + P], ident_bf[:], tri_key[:],
                                          start=False, stop=True)
                    elif kind == "strided":
                        ahead = j * STRIP - c * P * STRIDE
                        partly = -STRIP < ahead < P * STRIDE
                        m = pe.matmul(o, k.tile[:, h, c * P * STRIDE + STRIDE - 1:(c + 1) * P * STRIDE:STRIDE],
                                      q.tile[:, h, :], start=True, stop=not partly)
                        if partly:
                            m = pe.matmul(o, ident_h[:], mask_k[:, ahead:ahead + STRIP], start=False, stop=True)
                    else:
                        pe.matmul(o, ident_h[:], tri0_k[:], start=True, stop=False)
                        for b in range(BLOCKS):
                            at = j * STRIP + b * P
                            m = pe.matmul(slot.tile[:, i, b * P:(b + 1) * P], k.tile[:, h, at:at + P],
                                          q.tile[:, h, b * P:(b + 1) * P], start=False, stop=(b == BLOCKS - 1))
                    return m

                def exponent(slot, scored, first_col, hidden):
                    p, p_free = probs.take()
                    w_act(scored, *p_free)
                    extra = {"bias": after_bias[:, 0:1]} if hidden else {}
                    p.ready = A(act.activation(p.tile[:, :, first_col:STRIP], slot.tile[:, :, first_col:STRIP],
                                               ACT.Exp, scale=SCALE, **extra))
                    slot.readers.append(p.ready)
                    return p

                def weigh(kind, c, pair_probs, first_col, first, last):
                    w_pe(v.ready, *[p.ready for p in pair_probs], *(pv_free if first else []))
                    if sparse:
                        w_pe(sv.ready)
                    for b in (range(BLOCKS) if kind == "local" else (None,)):
                        for h in range(GROUP):
                            probs_tile = pair_probs[h // 2].tile
                            rows = slice(h * GCOL, (h + 1) * GCOL)
                            if kind == "local":
                                cols = slice(b * P, (b + 1) * P)
                                vt = v.tile[:, BLOCKS * j + b, rows]
                            else:
                                cols = slice(first_col, STRIP)
                                vt = (sv if kind == "strided" else v).tile[:, c, rows]
                            m = pe.matmul(pv.tile[rows, cols], vt, probs_tile[:, h % 2, cols], start=first,
                                          stop=(last and b in (None, BLOCKS - 1)), skip_group_check=True)
                    m = T(m)
                    for p in pair_probs:
                        p.readers.append(m)
                    return m

                def tile_step(n, kind, c):
                    first_col = max(0, c - BLOCKS * j) * P if kind == "dense" else 0
                    held = []

                    taken = []

                    def head_run(h):
                        def run():
                            if h % 2 == 0:
                                slot, readers = score_pairs.take()
                                w_pe(q.ready, keys_ready(k, u), *readers)
                                taken.append(slot)
                            scored = score(kind, c, taken[-1], h, first_col)
                            if h % 2 == 1:
                                hidden = kind == "strided" and j * STRIP - c * P * STRIDE <= -STRIP
                                held.append(exponent(taken[-1], T(scored), first_col, hidden))
                        return run

                    def weigh_run():
                        waiting.append((kind, c, held, first_col, n == 0, n == len(tiles) - 1))
                        if len(waiting) > 1:
                            weigh(*waiting.pop(0))
                    return [head_run(h) for h in range(GROUP)] + [weigh_run]

                for n, (kind, c) in enumerate(tiles):
                    steps += tile_step(n, kind, c)

                handed = []

                def finish():
                    while waiting:
                        m = weigh(*waiting.pop(0))
                    q.readers.append(m)
                    if u in last_of_group:
                        for s in (k, v) + ((sv,) if sparse else ()):
                            s.readers.append(m)
                    o, o_free = outs.take()
                    w_act(m, *o_free)
                    m = A(act.activation(o.tile[:], pv.tile, ACT.Copy))
                    pv.readers.append(m)
                    handed.append((o, m))

                def output():
                    o, m = handed[0]
                    bank, readers = side_banks.take()
                    w_pe(m, *readers)
                    for b in range(BLOCKS):
                        m = pe.transpose(bank.tile[:, b * P:(b + 1) * P], o.tile[:, b * P:(b + 1) * P], ident[:])
                    m = T(m)
                    o.readers.append(m)
                    turned = bank.tile.rearrange("p (b h n) -> p b h n", b=BLOCKS, n=GCOL)
                    r, r_free = recips.take()
                    ao, ao_free = aos.take()
                    w_dve(m, *r_free, *ao_free)
                    w_dve(V(dve.reciprocal(r.tile[:], turned[:, :, :, HEAD_DIM])))
                    m = V(dve.tensor_tensor(
                        ao.tile[:].rearrange("p b (h n) -> p b h n", h=GROUP), turned[:, :, :, 0:HEAD_DIM],
                        r.tile[:].unsqueeze(3).broadcast_to([P, BLOCKS, GROUP, HEAD_DIM]), ALU.mult))
                    bank.readers.append(m)
                    r.readers.append(m)
                    w_sp(m)
                    cols = slice(g * GROUP * HEAD_DIM, (g + 1) * GROUP * HEAD_DIM)
                    ao.readers.append(ao.store_signal.mark(sp.dma_start(rows_of(ao_d[a], j)[:, :, cols], ao.tile[:]), 16))
                steps.append(finish)
                return steps, output

            last_of_group = set(units[STRIPS - 1::STRIPS])

            size = [NSTR // P + 1 if sparse else BLOCKS * (j + 1) for _, _, j in units]

            def lead(n):
                if sparse:
                    return size[0] + 2
                if n >= len(units) - STRIPS:
                    return size[n] + 4
                return min(max(size) + 4, 10 + (2 * BLOCKS * done) ** 0.5)

            ahead = []
            if sparse:
                load_keys(units[0])
                load_queries(units[0])
            else:
                load_keys(units[0], slice(0, STRIP))
                load_queries(units[0])
                load_keys(units[0], slice(STRIP, TOKENS))
            load_values(units[0])
            late = None
            for n, u in enumerate(units):
                u_steps, hand_over = max_steps(u)
                if n + 1 < len(units):
                    ahead.append((0, None, lambda nxt=units[n + 1]: load_queries(nxt)))
                for i, step in enumerate(u_steps):
                    ahead.append((size[n] / len(u_steps), None, step))
                    if late and i == 4:
                        ahead.append(late)
                late = (0, u, hand_over)
            ahead.append(late)
            done_ahead, done, at = 0.0, 0.0, 0
            handed_over = set()

            def run_ahead(goal):
                nonlocal done_ahead, at
                while at < len(ahead) and done_ahead < goal:
                    work, unit, step = ahead[at]
                    step()
                    done_ahead += work
                    handed_over.add(unit)
                    at += 1

            output = None
            for n, u in enumerate(units):
                run_ahead(done + lead(n))
                while u not in handed_over:
                    run_ahead(done_ahead + 1e-6)
                main, next_output = attend_steps(u)
                if output:
                    main.insert(9, output)
                output = next_output
                if n < len(beside):
                    beside[n]()
                for step in main:
                    step()
                    done += size[n] / len(main)
                    run_ahead(done + lead(n))
                nxt = STRIPS if n == 0 else n + 1 + STRIPS
                if (n == 0 or u in last_of_group) and nxt < len(units):
                    load_keys(units[nxt])
                    load_values(units[nxt])
            output()
        everyone_waits()

    middle_early = ExitStack()
    staging = ring(middle_early, "stage3_", 2, [P, 3 * DIM], loads=True)
    attend((0,), "sparse", beside=[
        step for name, src, n_out in (("wproj0", d["L0_attn_c_proj_w"], DIM), ("w_rotary", d["L1_attn_Wqkv"], 3 * DIM),
                                      ("w_moe_qkv", d["moe_qkv"], 3 * DIM))
        for step in matrix(middle_early, staging, name, src, DIM, n_out)])


    with middle_early, ExitStack() as st3:
        weights = signal("middle_weights")
        n1 = sbuf(st3, "n1", [P, DIM])
        qkw = sbuf(st3, "qk_norm_w", [P, 2, HEAD_DIM])
        cos = sbuf(st3, "cos", [P, TOKENS // P, HEAD_DIM])
        sin = sbuf(st3, "sin", [P, TOKENS // P, HEAD_DIM])
        xs = ring(st3, "base_in", 2, [P, BLOCKS, DIM], loads=True, stores=True)
        aos = ring(st3, "ao_in", 2, [P, BLOCKS, DIM], loads=True)

        def load_mid(strip):
            got = []
            for r, src in ((xs, base_d), (aos, ao_d[0])):
                slot, readers = r.take()
                w_sp(*readers)
                slot.ready = slot.load_signal.mark(sp.dma_start(slot.tile[:], rows_of(src, strip)), 16)
                got.append(slot)
            return got

        loaded = [load_mid(0)]
        wproj, wr, wf = w["wproj0"], w["w_rotary"], w["w_moe_qkv"]
        for tile, src in ((n1[:], d["L1_ffn_n1_w"].partition_broadcast(P)),
                          (qkw[:, 0, :], d["L1_ffn_qn_w"].partition_broadcast(P)),
                          (qkw[:, 1, :], d["L1_ffn_kn_w"].partition_broadcast(P)),
                          (cos[:], d["c_cos"]), (sin[:], d["c_sin"])):
            w_in = weights.mark(sp.dma_start(tile, src), 16)
        aots = split_ring(st3, "aot", 1, [P, DC, STRIP])
        xns = ring(st3, "xn1_s", 2, [P, BLOCKS, DIM], stores=True)
        hs = ring(st3, "h_s", 1, [P, BLOCKS, DIM])
        xts = split_ring(st3, "xt1", 2, [P, DC, STRIP])
        qkns = ring(st3, "qkn1_s", 3, [P, BLOCKS, QK])
        ves = ring(st3, "ve1_s", 2, [P, BLOCKS, HEADS * GCOL], stores=True)
        stats = (sbuf(st3, "ln1_stats", [P, BLOCKS, 6]), sbuf(st3, "ln1_mv", [P, BLOCKS, 2]))
        small = sbuf(st3, "ln1_small", [P, 4, BLOCKS])
        ms = sbuf(st3, "ms1", [P, BLOCKS])
        junk = sbuf(st3, "junk1", [P, DIM])
        rots = ring(st3, "rot", 2, [P, QK])
        turns = ring(st3, "turn", 2, [P, QK])
        hsqs = ring(st3, "head_squares", 2, [P, QK])
        hms_ring = ring(st3, "head_ms", 2, [P, BLOCKS, 2 * HEADS])
        hsmall = sbuf(st3, "head_small", [P, 4, BLOCKS * 2 * HEADS])
        parts_ring = parts_buffers(st3, "part1_", 2)
        for slot in ves.slots:
            slot.ready = G(pool.memset(slot.tile[:], 1.0))
        pairs, qk_banks, v_banks = pair_ring((0, 2)), bank_ring((4, 5)), bank_ring((6, 7))
        state = {}

        def turn_attention(strip):
            if strip + 1 < STRIPS:
                loaded.append(load_mid(strip + 1))
            ao = loaded[strip][1]
            aot, aot_free = aots.take()
            aot_ready, read = to_split_features(ao.tile, ao.ready, pairs, aot, aot_free)
            ao.readers.append(read)
            state[strip] = dict(aot=aot, aot_ready=aot_ready)

        def residual(strip):
            x, aot = loaded[strip][0], state[strip]["aot"]
            w_pe(state[strip]["aot_ready"], w["wproj0_ready"])
            w_dve(x.ready)
            for half in range(BLOCKS // 2):
                bank, readers = v_banks.take()
                w_pe(*readers)
                for b in (2 * half, 2 * half + 1):
                    m_mm = T(product(bank.tile[:, b % 2 * DIM:(b % 2 + 1) * DIM],
                                     lambda l, c: aot.tile[l][:, c, b * P:(b + 1) * P], lambda r, c: wproj[r][:, c, :], DC))
                w_dve(m_mm)
                x_half = x.tile[:, 2 * half:2 * half + 2, :]
                m = V(dve.tensor_tensor(x_half, x_half, bank.tile.rearrange("p (b n) -> p b n", b=2), ALU.add))
                bank.readers.append(m)
            aot.readers.append(m_mm)
            w_dve(m)
            w_sp(m)
            x.readers.append(x.store_signal.mark(sp.dma_start(rows_of(x1_d, strip), x.tile[:]), 16))
            xn, xn_free = xns.take()
            w_dve(*xn_free)
            normed = layer_norm(x.tile, xn.tile, stats, small)
            x.readers.append(normed)
            w_sp(normed)
            xn.readers.append(xn.store_signal.mark(sp.dma_start(rows_of(xn_d, strip), xn.tile[:]), 16))
            state[strip].update(xn=xn, normed=normed)

        def rms(strip):
            xn = state[strip]["xn"]
            h, h_free = hs.take()
            w_dve(state[strip]["normed"], w_in)
            mean_square(xn.tile, junk, ms)
            rs, _ = norm_scale(small, ms[:], RMS_EPS)
            w_dve(*h_free)
            for b in range(BLOCKS):
                m = V(dve.scalar_tensor_tensor(out=h.tile[:, b, :], in0=xn.tile[:, b, :], scalar=rs[:, b:b + 1],
                                               in1=n1[:], op0=ALU.mult, op1=ALU.mult))
            xn.readers.append(m)
            state[strip].update(h=h, h_normed=m)

        def turn(strip):
            st = state[strip]
            for name, src, ready in (("xt", "xn", "normed"), ("ht", "h", "h_normed")):
                st[name], free = xts.take()
                st[name + "_ready"], read = to_split_features(st[src].tile, st[ready], pairs, st[name], free)
                st[src].readers.append(read)

        def projections(a, xt, xt_ready, w, on_qk):
            ve, ve_free = ves.take()
            w_pe(xt_ready)
            w_act(*ve_free, ve.ready)
            for b in range(BLOCKS):
                tok = slice(b * P, (b + 1) * P)
                bank, readers = qk_banks.take()
                w_pe(*readers)
                m = T(product(bank.tile, lambda l, c: xt.tile[l][:, c, tok], lambda r, c: w[r][:, c, 0:QK], DC))
                on_qk(b, bank, m)
                if b % 2 == 0:
                    vbank, readers = v_banks.take()
                    w_pe(*readers)
                m_mm = T(product(vbank.tile[:, b % 2 * DIM:(b % 2 + 1) * DIM], lambda l, c: xt.tile[l][:, c, tok],
                                 lambda r, c: w[r][:, c, QK:QK + DIM], DC))
                if b % 2 == 1:
                    w_act(m_mm)
                    for i in (b - 1, b):
                        m_v = A(act.activation(v_columns(ve.tile, i)[:, 0],
                                               vbank.tile[:, i % 2 * DIM:(i % 2 + 1) * DIM].rearrange("p (h n) -> p h n", n=HEAD_DIM), ACT.Copy))
                    vbank.readers.append(m_v)
            xt.readers.append(m_mm)
            return ve, m_v

        def rotary(strip):
            st = state[strip]
            qkn, qkn_free = qkns.take()
            w_pool(*qkn_free)
            w_dve(*qkn_free)

            def on_qk(b, bank, m):
                blk = strip * BLOCKS + b
                turn_t, turn_free = turns.take()
                rot_t, rot_free = rots.take()
                w_dve(m, *turn_free, *rot_free)
                q4 = bank.tile.rearrange("p (h n two) -> p h n two", h=2 * HEADS, two=2)
                t4 = turn_t.tile[:].rearrange("p (h n two) -> p h n two", h=2 * HEADS, two=2)
                s4 = sin[:, blk, :].rearrange("p (n two) -> p n two", two=2)
                for two in range(2):
                    V(dve.tensor_tensor(t4[:, :, :, two], q4[:, :, :, 1 - two],
                                        s4[:, :, two].unsqueeze(1).broadcast_to([P, 2 * HEADS, HEAD_DIM // 2]), ALU.mult))
                m = V(dve.tensor_tensor(
                    rot_t.tile[:].rearrange("p (h n) -> p h n", n=HEAD_DIM), bank.tile.rearrange("p (h n) -> p h n", n=HEAD_DIM),
                    cos[:, blk, :].unsqueeze(1).broadcast_to([P, 2 * HEADS, HEAD_DIM]), ALU.mult))
                bank.readers.append(m)
                w_pool(m)
                st["rot_ready"] = G(pool.tensor_tensor(qkn.tile[:, b, :], rot_t.tile[:], turn_t.tile[:], ALU.add))
                turn_t.readers.append(st["rot_ready"])
                rot_t.readers.append(st["rot_ready"])

            ve, m_v = projections(1, st["xt"], st["xt_ready"], wr, on_qk)
            ve.readers.append(store_v(1, strip, ve, m_v))
            st["rot"] = qkn

        def parts(strip, a, qkn, ready):
            slot, parts_free = parts_ring.take()
            turned, kept = make_parts(a, strip, qkn.tile, ready, pairs, slot, parts_free)
            slot.readers.append(kept)
            qkn.readers.append(turned)

        def head_norm(strip):
            st = state[strip]
            hms, hms_free = hms_ring.take()
            reduces = []
            st["hms"] = hms
            qkn, qkn_free = qkns.take()
            w_act(*qkn_free)

            def on_qk(b, bank, m):
                w_act(m)
                m = A(act.activation(qkn.tile[:, b, :], bank.tile, ACT.Copy))
                bank.readers.append(m)
                sq, sq_free = hsqs.take()
                w_pool(m, *sq_free)
                squared = G(pool.tensor_tensor(sq.tile[:], qkn.tile[:, b, :], qkn.tile[:, b, :], ALU.mult))
                w_dve(*hms_free)
                if b == 2 and strip + 1 < STRIPS:
                    rms(strip + 1)
                if b == 3 and strip > 0:
                    scale_heads(strip - 1)
                w_dve(squared)
                m = V(dve.tensor_reduce(hms.tile[:, b, :], sq.tile[:].rearrange("p (h n) -> p h n", n=HEAD_DIM), AX.X, ALU.add))
                sq.readers.append(m)
                st["squared"] = m

            ve, m_v = projections(2, st["ht"], st["ht_ready"], wf, on_qk)
            ve.readers.append(store_v(2, strip, ve, m_v))
            st["heads"] = qkn

        def scale_heads(strip):
            st = state[strip]
            qkn = st["heads"]
            hms_flat = st["hms"].tile[:].rearrange("p b h -> p (b h)")
            w_dve(st["squared"])
            w_dve(V(dve.tensor_scalar(hms_flat, hms_flat, 1.0 / HEAD_DIM, None, ALU.mult)))
            rs, scaled = norm_scale(hsmall, hms_flat, RMS_EPS)
            st["hms"].readers.append(scaled)
            q3 = qkn.tile[:].rearrange("p b (h n) -> p (b h) n", n=HEAD_DIM)
            m = V(dve.tensor_tensor(q3, q3, rs.unsqueeze(2).broadcast_to([P, BLOCKS * 2 * HEADS, HEAD_DIM]), ALU.mult))
            w_pool(m, w_in)
            for i in range(2):
                q4 = qkn.tile[:, :, i * DIM:(i + 1) * DIM].rearrange("p b (h n) -> p b h n", n=HEAD_DIM)
                for b in range(BLOCKS):
                    m = G(pool.tensor_tensor(q4[:, b], q4[:, b],
                                             qkw[:, i, :].unsqueeze(1).broadcast_to([P, HEADS, HEAD_DIM]), ALU.mult))
            st["heads_ready"] = m

        turn_attention(0)
        residual(0)
        rms(0)
        turn(0)
        w_pe(w["w_rotary_ready"], w["w_moe_qkv_ready"])
        for strip in range(STRIPS):
            st = state[strip]
            more = strip + 1 < STRIPS
            if more:
                turn_attention(strip + 1)
            rotary(strip)
            if more:
                residual(strip + 1)
            head_norm(strip)
            if more:
                turn(strip + 1)
            parts(strip, 1, st["rot"], st["rot_ready"])
            if not more:
                scale_heads(strip)
            if strip > 0:
                parts(strip - 1, 2, state[strip - 1]["heads"], state[strip - 1]["heads_ready"])
        parts(STRIPS - 1, 2, state[STRIPS - 1]["heads"], state[STRIPS - 1]["heads_ready"])
    everyone_waits()

    HID = 512
    early = ctx.enter_context(ExitStack())
    staging = ring(early, "stage5_", 2, [P, HID], loads=True)

    final_weights = signal("final_weights")
    wp = sbuf(early, "wproj1", [P, DC, DIM])
    wo = sbuf(early, "wo", [P, DC, KEPT])
    n2 = sbuf(early, "n2", [P, DIM])
    lower = sbuf(early, "lower", [P, EXPERTS, EXPERTS])
    for tile, src in ((wo[:], d["L1_ffn_wo"].rearrange("(c p) n -> p c n", p=P)[:, :, MASKED:DIM]),
                      (wp[:], d["L1_attn_Wproj"].rearrange("(c p) n -> p c n", p=P)),
                      (n2[:], d["L1_ffn_n2_w"].partition_broadcast(P)), (lower[:], d["c_lower"])):
        final_in = final_weights.mark(sp.dma_start(tile, src), 16)
    attend((1, 2), "dense", beside=[
        step for name, n_out in (("gate_w", EXPERTS), ("e0_up", HID), ("e2_l1", HID), ("e1_w1", HID), ("e1_w2", HID))
        for step in matrix(early, staging, name, d["L1_ffn_" + name], DIM, n_out)])


    with ExitStack() as st5:
        aos = ring(st5, "ao_last_in", 2, [P, BLOCKS, DIM], loads=True)
        x1s = ring(st5, "x1_in", 1, [P, BLOCKS, DIM], loads=True)
        xas = ring(st5, "xa_in", 2, [P, BLOCKS, DIM], loads=True, stores=True)

        def load_end(strip):
            got = []
            for r, src in ((aos, ao_d[2]), (xas, xn_d), (aos, ao_d[1]), (x1s, x1_d)):
                slot, readers = r.take()
                w_sp(*readers)
                slot.ready = slot.load_signal.mark(sp.dma_start(slot.tile[:], rows_of(src, strip)), 16)
                got.append(slot)
            return got

        loaded = {0: load_end(0)}
        xfs = ring(st5, "xf", 1, [P, BLOCKS, DIM])
        a_ts = ring(st5, "a_t", 2, [P, DC, STRIP])
        xfts = split_ring(st5, "xft", 1, [P, DC, STRIP])
        hids = split_ring(st5, "hid", 3, [P, HID // P, STRIP])
        gs = ring(st5, "activated", 2, [P, STRIP])
        small = sbuf(st5, "rms_small", [P, 4, BLOCKS])
        ms = sbuf(st5, "ms5", [P, BLOCKS])
        junk = sbuf(st5, "junk5", [P, DIM])
        logit = sbuf(st5, "logit", [P, BLOCKS, EXPERTS])
        prob = sbuf(st5, "prob", [P, BLOCKS, EXPERTS])
        red = sbuf(st5, "red", [P, BLOCKS, 4])
        beats = sbuf(st5, "beats", [P, BLOCKS, EXPERTS, EXPERTS])
        ties = sbuf(st5, "ties", [P, BLOCKS, EXPERTS, EXPERTS])
        rank = sbuf(st5, "rank", [P, BLOCKS, EXPERTS])
        wts_ring = ring(st5, "wts", 2, [P, BLOCKS, EXPERTS])
        turn_pair, o_banks, h_banks = pair_ring((0,)), bank_ring((2, 3)), bank_ring((4, 5, 6, 7))
        w_dve(final_in)
        w_pe(final_in)
        state = {}
        later_weights = [step for name, n_in, n_out, first_col in (
            ("e0_down", HID, DIM, MASKED), ("e2_l2", HID, HID, 0), ("e1_down", HID, DIM, MASKED), ("e3_down", DIM, DIM, 0),
            ("e2_l3", HID, HID, 0), ("e3_up", DIM, HID, 0), ("e2_l4", HID, DIM, MASKED), ("e3_out", HID, DIM, MASKED))
            for step in matrix(st5, staging, name, d["L1_ffn_" + name], n_in, n_out, first_col)]

        def bcast(ap, n):
            return ap.unsqueeze(2).broadcast_to([P, BLOCKS, n])

        def combine(strip):
            ao2, xa, ao1, x1 = loaded.pop(strip)
            a2t, a2t_free = a_ts.take()
            t2, read = to_features(ao2.tile, ao2.ready, turn_pair, a2t.tile, a2t_free)
            ao2.readers.append(read)
            a1t, a1t_free = a_ts.take()
            t1, read = to_features(ao1.tile, ao1.ready, turn_pair, a1t.tile, a1t_free)
            ao1.readers.append(read)
            w_pe(t1, t2)
            w_dve(x1.ready, xa.ready)
            for half in range(BLOCKS // 2):
                bank, readers = o_banks.take()
                w_pe(*readers)
                for b in (2 * half, 2 * half + 1):
                    for c in range(DC):
                        m = pe.matmul(bank.tile[:, b % 2 * KEPT:(b % 2 + 1) * KEPT], a2t.tile[:, c, b * P:(b + 1) * P],
                                      wo[:, c, :], start=(c == 0), stop=(c == DC - 1))
                m_mm = T(m)
                w_dve(m_mm)
                kept = xa.tile[:, 2 * half:2 * half + 2, MASKED:DIM]
                m = V(dve.tensor_tensor(kept, kept, bank.tile[:, 0:2 * KEPT].rearrange("p (b n) -> p b n", b=2), ALU.add))
                bank.readers.append(m)
            a2t.readers.append(m_mm)
            w_dve(m)
            mean_square(xa.tile, junk, ms)
            rs, _ = norm_scale(small, ms[:], RMS_EPS)
            xf, xf_free = xfs.take()
            w_dve(*xf_free)
            for b in range(BLOCKS):
                normed = V(dve.scalar_tensor_tensor(out=xf.tile[:, b, :], in0=xa.tile[:, b, :], scalar=rs[:, b:b + 1],
                                                    in1=n2[:], op0=ALU.mult, op1=ALU.mult))
            for half in range(BLOCKS // 2):
                bank, readers = o_banks.take()
                w_pe(*readers)
                for b in (2 * half, 2 * half + 1):
                    for c in range(DC):
                        m = pe.matmul(bank.tile[:, b % 2 * DIM:(b % 2 + 1) * DIM], a1t.tile[:, c, b * P:(b + 1) * P],
                                      wp[:, c, :], start=(c == 0), stop=(c == DC - 1))
                m_mm = T(m)
                w_dve(m_mm)
                x_half = x1.tile[:, 2 * half:2 * half + 2, :]
                m = V(dve.tensor_tensor(x_half, x_half, bank.tile.rearrange("p (b n) -> p b n", b=2), ALU.add))
                bank.readers.append(m)
            a1t.readers.append(m_mm)
            w_dve(m)
            m_sum = V(dve.tensor_tensor(xa.tile[:], xa.tile[:], x1.tile[:], ALU.add))
            x1.readers.append(m_sum)
            state[strip] = dict(xa=xa, summed=m_sum, xf=xf, normed=normed)

        def turn(strip):
            st = state[strip]
            st["xft"], free = xfts.take()
            st["xft_ready"], read = to_split_features(st["xf"].tile, st["normed"], turn_pair, st["xft"], free)
            st["xf"].readers.append(read)

        def router(strip):
            st = state[strip]
            xft = st["xft"].tile
            st["wts"], wts_free = wts_ring.take()
            wts = st["wts"].tile
            bank, readers = o_banks.take()
            w_pe(st["xft_ready"], w["gate_w_ready"], *readers)
            for b in range(BLOCKS):
                m = product(bank.tile[:, b * EXPERTS:(b + 1) * EXPERTS], lambda l, c: xft[l][:, c, b * P:(b + 1) * P],
                            lambda r, c: w["gate_w"][r][:, c, :], DC)
            w_dve(T(m), (dve_done, dve_done.count))
            big = 3.4028234663852886e38
            m = V(dve.tensor_scalar(logit[:].rearrange("p b e -> p (b e)"), bank.tile[:, 0:BLOCKS * EXPERTS],
                                    big, -big, ALU.min, ALU.max))
            bank.readers.append(m)
            w_dve(m)
            w_dve(V(dve.tensor_reduce(red[:, :, 0], logit[:], AX.X, ALU.max)))
            m = V(dve.tensor_tensor(logit[:], logit[:], bcast(red[:, :, 0], EXPERTS), ALU.subtract))
            w_act(m)
            w_dve(A(act.activation(prob[:], logit[:], ACT.Exp)))
            w_dve(V(dve.tensor_reduce(red[:, :, 1], prob[:], AX.X, ALU.add)))
            w_dve(V(dve.reciprocal(red[:, :, 2], red[:, :, 1])))
            w_dve(V(dve.tensor_tensor(prob[:], prob[:], bcast(red[:, :, 2], EXPERTS), ALU.mult)))
            other = prob[:].unsqueeze(2).broadcast_to([P, BLOCKS, EXPERTS, EXPERTS])
            own = prob[:].unsqueeze(3).broadcast_to([P, BLOCKS, EXPERTS, EXPERTS])
            for b in range(BLOCKS):
                V(dve.tensor_tensor(beats[:, b], other[:, b], own[:, b], ALU.is_gt))
                w_dve(V(dve.tensor_tensor(ties[:, b], other[:, b], own[:, b], ALU.is_equal)))
                m = V(dve.tensor_tensor(ties[:, b], ties[:, b], lower[:], ALU.mult))
            w_dve(m)
            flat = "p b e f -> p (b e f)"
            w_dve(V(dve.tensor_tensor(beats[:].rearrange(flat), beats[:].rearrange(flat), ties[:].rearrange(flat), ALU.add)))
            w_dve(V(dve.tensor_reduce(rank[:], beats[:], AX.X, ALU.add)), *wts_free)
            w_dve(V(dve.scalar_tensor_tensor(out=wts[:], in0=rank[:], scalar=1.5, in1=prob[:], op0=ALU.is_lt, op1=ALU.mult)))
            w_dve(V(dve.tensor_reduce(red[:, :, 0], wts[:], AX.X, ALU.add)))
            w_dve(V(dve.tensor_scalar(red[:, :, 0], red[:, :, 0], 1e-8, None, ALU.add)))
            w_dve(V(dve.reciprocal(red[:, :, 1], red[:, :, 0])))
            st["total"] = V(dve.tensor_tensor(wts[:], wts[:], bcast(red[:, :, 1], EXPERTS), ALU.mult))

        def hidden(src, src_ready, name, n_in, n_out, func, gate=None):
            slot, free = hids.take()
            high, low = slot.tile
            for f in range(n_out // P):
                cols = slice(f * P, (f + 1) * P)
                bank, readers = h_banks.take()
                w_pe(src_ready, w[name + "_ready"], *readers)
                m = T(product(bank.tile, lambda l, c: w[name][l][:, c, cols], lambda r, c: src[r][:, c, :], n_in // P))
                g, g_free = gs.take()
                w_act(m, *g_free)
                m = A(act.activation(g.tile[:], bank.tile, func))
                bank.readers.append(m)
                w_dve(m, *free)
                if gate:
                    bank, readers = h_banks.take()
                    w_pe(w[gate + "_ready"], *readers)
                    w_dve(T(product(bank.tile, lambda l, c: w[gate][l][:, c, cols], lambda r, c: src[r][:, c, :], n_in // P)))
                    m = V(dve.tensor_tensor(g.tile[:], g.tile[:], bank.tile, ALU.mult))
                    bank.readers.append(m)
                    w_dve(m)
                w_dve(V(dve.tensor_copy(high[:, f, :], g.tile[:])))
                m = V(dve.tensor_tensor(low[:, f, :], g.tile[:], high[:, f, :].bitcast(F32), ALU.subtract))
                g.readers.append(m)
            return slot, m

        def expert_out(st, e, hid, ready, name):
            wts, total = st["wts"].tile, st["xa"].tile
            w_dve(st["total"], st["summed"])
            for b in range(BLOCKS):
                bank, readers = o_banks.take()
                w_pe(ready, w[name + "_ready"], *readers)
                m_mm = T(product(bank.tile[:, 0:KEPT], lambda l, c: hid.tile[l][:, c, b * P:(b + 1) * P],
                                 lambda r, c: w[name][r][:, c, :], HID // P))
                w_dve(m_mm)
                total_b = total[:, b, MASKED:DIM]
                m = V(dve.scalar_tensor_tensor(out=total_b, in0=bank.tile[:, 0:KEPT], scalar=wts[:, b, e:e + 1],
                                               in1=total_b, op0=ALU.mult, op1=ALU.add))
                bank.readers.append(m)
            hid.readers.append(m_mm)
            st["total"] = m

        def pe_now():
            return (pe_done, pe_done.count)

        for step in later_weights[0:8]:
            step()
        combine(0)
        loaded[1] = load_end(1)
        for step in later_weights[8:]:
            step()
        turn(0)
        router(0)
        for strip in range(STRIPS):
            st = state[strip]
            x_t, x_ready = st["xft"].tile, st["xft_ready"]
            first = strip == 0
            h0, m0 = hidden(x_t, x_ready, "e0_up", DIM, HID, ACT.Gelu)
            g1, mg1 = hidden(x_t, x_ready, "e2_l1", DIM, HID, ACT.Gelu)
            s1, ms1 = hidden(x_t, x_ready, "e1_w1", DIM, HID, ACT.Silu, gate="e1_w2")
            expert_out(st, 0, h0, m0, "e0_down")
            g2, mg2 = hidden(g1.tile, mg1, "e2_l2", HID, HID, ACT.Gelu)
            g1.readers.append(pe_now())
            expert_out(st, 1, s1, ms1, "e1_down")
            r1, mr1 = hidden(x_t, x_ready, "e3_down", DIM, DIM, ACT.Gelu)
            st["xft"].readers.append(pe_now())
            if not first and strip + 1 < STRIPS:
                combine(strip + 1)
            g3, mg3 = hidden(g2.tile, mg2, "e2_l3", HID, HID, ACT.Gelu)
            g2.readers.append(pe_now())
            r2, mr2 = hidden(r1.tile, mr1, "e3_up", DIM, HID, ACT.Gelu)
            r1.readers.append(pe_now())
            if first:
                combine(strip + 1)
            if strip + 1 < STRIPS:
                turn(strip + 1)
            expert_out(st, 2, g3, mg3, "e2_l4")
            if strip + 1 < STRIPS:
                router(strip + 1)
            expert_out(st, 3, r2, mr2, "e3_out")
            st["wts"].readers.append(st["total"])
            w_sp(st["total"])
            st["xa"].readers.append(st["xa"].store_signal.mark(sp.dma_start(rows_of(out, strip), st["xa"].tile[:]), 16))
            if strip + 2 < STRIPS:
                loaded[strip + 2] = load_end(strip + 2)
    everyone_waits()


_TRANSPOSED = ("L1_ffn_wo", "L1_ffn_gate_w", "L1_ffn_e0_up", "L1_ffn_e0_down",
               "L1_ffn_e1_w1", "L1_ffn_e1_w2", "L1_ffn_e1_down", "L1_ffn_e2_l1", "L1_ffn_e2_l2", "L1_ffn_e2_l3",
               "L1_ffn_e2_l4", "L1_ffn_e3_down", "L1_ffn_e3_up", "L1_ffn_e3_out")
_PLAIN = ("L0_attn_c_attn_w", "L0_attn_c_attn_b", "L0_attn_c_proj_w", "L0_attn_c_proj_b", "L0_ffn_kernel",
          "L0_ffn_input_scale", "L0_ffn_kernel_scale", "L0_ffn_bias", "L1_attn_Wqkv", "L1_attn_Wproj",
          "L1_ffn_n1_w", "L1_ffn_n2_w", "L1_ffn_qn_w", "L1_ffn_kn_w")


def shape_constants(bf16):
    part = np.arange(P)[:, None]
    col = np.arange(P)[None, :]
    key_after = (part > col)
    own = np.arange(P // STRIDE)[None, :]
    ahead = np.arange(2 * P * STRIDE - STRIP)[None, :]
    inv = (np.float32(1.0) / np.float32(10000.0) ** (np.arange(0, HEAD_DIM, 2, dtype=np.float32) / np.float32(HEAD_DIM)))
    angle = np.arange(TOKENS, dtype=np.float32)[:, None] * inv.astype(np.float32)[None, :]
    cos = np.repeat(np.cos(angle), 2, axis=-1).astype(np.float32)
    sin = np.repeat(np.sin(angle), 2, axis=-1).astype(np.float32)
    sin[:, 0::2] *= -1
    by_block = lambda t: np.ascontiguousarray(t.reshape(TOKENS // P, P, HEAD_DIM).transpose(1, 0, 2))
    lower = np.tile((np.arange(EXPERTS)[None, :] < np.arange(EXPERTS)[:, None])[None], (P, 1, 1))
    return {
        "c_ident": np.eye(P, dtype=np.float32),
        "c_ident_bf": np.eye(P, dtype=np.float32).astype(bf16),
        "c_ident_h": np.eye(P, dtype=np.float16),
        "c_tri_key": (key_after * np.float32(NEG1)).astype(bf16),
        "c_tri_query": (key_after.T * np.float32(NEG1)).astype(bf16),
        "c_tri0_k": np.tile(key_after * NEG0, (1, BLOCKS)).astype(np.float16),
        "c_tri0_q": np.tile(key_after.T * NEG0, (1, GROUP)).astype(np.float16),
        "c_mask_q": ((STRIDE * own + STRIDE - 1 > part) * NEG0).astype(np.float16),
        "c_mask_k": ((STRIDE * part + STRIDE - 1 > ahead) * NEG0).astype(np.float16),
        "c_ones": np.ones((MROWS, GROUP, TOKENS), dtype=bf16),
        "c_cos": by_block(cos), "c_sin": by_block(sin), "c_lower": lower.astype(np.float32),
    }


def kernel(**inputs):
    import concourse.bacc as _bacc
    from concourse import mybir as _mybir
    from concourse.bass_utils import run_bass_kernel_spmd as _run

    nc = _bacc.Bacc("TRN2", target_bir_lowering=False, num_devices=1)
    host = {"L0_attn_hidden_states": np.asarray(inputs["L0_attn_hidden_states"]).reshape(TOKENS, DIM)}
    for name in _PLAIN:
        host[name] = np.asarray(inputs[name])
    for name in _TRANSPOSED:
        host[name] = np.asarray(inputs[name]).T
    host["bias_by_feature"] = np.asarray(inputs["L0_attn_c_attn_b"])[0:QK].reshape(QK // P, P).T
    host["moe_qkv"] = np.concatenate([np.asarray(inputs["L1_ffn_w" + n]).T for n in "qkv"], axis=1)
    host.update(shape_constants(host["L0_ffn_kernel"].dtype))
    arrays, args = {}, {}
    for name, a in host.items():
        a = np.ascontiguousarray(a)
        arrays[f"in_{name}"] = a
        args[name] = nc.dram_tensor(f"in_{name}", a.shape, _mybir.dt.from_np(a.dtype), kind="ExternalInput").ap()
    out = nc.dram_tensor("out_dram", (TOKENS, DIM), F32, kind="ExternalOutput").ap()
    build(nc, args, out)
    r = _run(nc, [arrays], core_ids=[0])
    return r.results[0]["out_dram"].reshape(1, TOKENS, DIM)
```
